# Optimizing a Trainium2 kernel written in Bass

```python
import numpy as np
import jax
import jax.numpy as jnp

def _softmax(x, axis=-1):
    return jax.nn.softmax(x, axis=axis)

def _gelu(x):
    return jax.nn.gelu(x, approximate=True)

def _silu(x):
    return jax.nn.silu(x)

def _sigmoid(x):
    return jax.nn.sigmoid(x)

def _layernorm(x, axis=-1, eps=1e-05):
    m = jnp.mean(x, axis=axis, keepdims=True)
    v = jnp.var(x, axis=axis, keepdims=True)
    return (x - m) / jnp.sqrt(v + eps)

def _scatter_add(tgt, idx, src, axis=0):
    return tgt.at[idx].add(src)

def _segment_sum(src, seg, n):
    return jax.ops.segment_sum(src, seg, n)
kernel_name = 'mk_adj_seq_d1_adj_r2_9c2efb'

def setup_inputs(seed: int=0):
    np.random.seed(seed)
    _w = jnp.asarray

    def _rec_inputs():
        import jax
        import jax.numpy as jnp
        _gk = jax.random.key(seed)
        x = -0.001547 + 1.001 * jax.random.normal(jax.random.fold_in(_gk, 1), (128, 64, 128), jnp.float32)
        _a = jax.random.bernoulli(jax.random.fold_in(_gk, 2), 0.125, (128, 64, 64))
        _a = jnp.logical_or(_a, jnp.swapaxes(_a, -1, -2))
        _a = jnp.logical_or(_a, jnp.eye(64, dtype=bool))
        _af = _a.astype(jnp.float32)
        _af = _af * jax.random.uniform(jax.random.fold_in(_gk, 3), (128, 64, 64), jnp.float32, 0.05, 0.99991)
        adj = _af
        return (x, adj)
    x, adj = _rec_inputs()

    def _L0_gnn_setup():
        import jax, jax.numpy as jnp
        import numpy as np
        B, N, D, H = (32, 64, 128, 128)
        LN_EPS = 1e-05

        def _mlp(x, W1, b1, g, beta, W2, b2):
            h = x @ W1 + b1
            mu = jnp.mean(h, axis=-1, keepdims=True)
            var = jnp.var(h, axis=-1, keepdims=True)
            h = (h - mu) * jax.lax.rsqrt(var + LN_EPS) * g + beta
            h = jax.nn.gelu(h, approximate=False)
            return h @ W2 + b2
        key = jax.random.key(seed)
        ks = jax.random.split(key, 10)
        s = lambda fan_in: 1.0 / np.sqrt(fan_in)
        return {'slots': jax.random.normal(ks[0], (B, N, D), dtype=jnp.float32), 'adjacency': jax.random.uniform(ks[1], (B, N, N), dtype=jnp.float32), 'We1': jax.random.uniform(ks[2], (2 * D, H), minval=-s(2 * D), maxval=s(2 * D), dtype=jnp.float32), 'be1': jnp.zeros((H,), jnp.float32), 'ge': jnp.ones((H,), jnp.float32), 'bge': jnp.zeros((H,), jnp.float32), 'We2': jax.random.uniform(ks[3], (H, D), minval=-s(H), maxval=s(H), dtype=jnp.float32), 'be2': jnp.zeros((D,), jnp.float32), 'Wn1': jax.random.uniform(ks[4], (2 * D, H), minval=-s(2 * D), maxval=s(2 * D), dtype=jnp.float32), 'bn1': jnp.zeros((H,), jnp.float32), 'gn': jnp.ones((H,), jnp.float32), 'bgn': jnp.zeros((H,), jnp.float32), 'Wn2': jax.random.uniform(ks[5], (H, D), minval=-s(H), maxval=s(H), dtype=jnp.float32), 'bn2': jnp.zeros((D,), jnp.float32)}
    _L0_gnn_all = _L0_gnn_setup()
    _L0_gnn_in = {k: v for k, v in _L0_gnn_all.items() if k in ('We1', 'be1', 'ge', 'bge', 'We2', 'be2', 'Wn1', 'bn1', 'gn', 'bgn', 'Wn2', 'bn2')}
    del _L0_gnn_all
    return {'x': x, 'adj': adj, 'L0_gnn_We1': _L0_gnn_in['We1'], 'L0_gnn_be1': _L0_gnn_in['be1'], 'L0_gnn_ge': _L0_gnn_in['ge'], 'L0_gnn_bge': _L0_gnn_in['bge'], 'L0_gnn_We2': _L0_gnn_in['We2'], 'L0_gnn_be2': _L0_gnn_in['be2'], 'L0_gnn_Wn1': _L0_gnn_in['Wn1'], 'L0_gnn_bn1': _L0_gnn_in['bn1'], 'L0_gnn_gn': _L0_gnn_in['gn'], 'L0_gnn_bgn': _L0_gnn_in['bgn'], 'L0_gnn_Wn2': _L0_gnn_in['Wn2'], 'L0_gnn_bn2': _L0_gnn_in['bn2']}

def reference(x, adj, L0_gnn_We1, L0_gnn_be1, L0_gnn_ge, L0_gnn_bge, L0_gnn_We2, L0_gnn_be2, L0_gnn_Wn1, L0_gnn_bn1, L0_gnn_gn, L0_gnn_bgn, L0_gnn_Wn2, L0_gnn_bn2):
    import jax
    import jax.numpy as jnp

    def _L0_gnn_ref(slots, adjacency, We1, be1, ge, bge, We2, be2, Wn1, bn1, gn, bgn, Wn2, bn2):
        import jax, jax.numpy as jnp
        import numpy as np
        B, N, D, H = (32, 64, 128, 128)
        LN_EPS = 1e-05

        def _mlp(x, W1, b1, g, beta, W2, b2):
            h = x @ W1 + b1
            mu = jnp.mean(h, axis=-1, keepdims=True)
            var = jnp.var(h, axis=-1, keepdims=True)
            h = (h - mu) * jax.lax.rsqrt(var + LN_EPS) * g + beta
            h = jax.nn.gelu(h, approximate=False)
            return h @ W2 + b2
        b, n, d = slots.shape
        ei = jnp.broadcast_to(slots[:, :, None, :], (b, n, n, d))
        ej = jnp.broadcast_to(slots[:, None, :, :], (b, n, n, d))
        edge_feat = jnp.concatenate([ei, ej], axis=-1)
        edge_out = _mlp(edge_feat, We1, be1, ge, bge, We2, be2)
        mask = 1.0 - jnp.eye(n, dtype=slots.dtype)
        w = adjacency * mask
        messages = jnp.einsum('bij,bijd->bid', w, edge_out)
        node_input = jnp.concatenate([slots, messages], axis=-1)
        delta = _mlp(node_input, Wn1, bn1, gn, bgn, Wn2, bn2)
        return slots + delta
    x = _L0_gnn_ref(x, adj, L0_gnn_We1, L0_gnn_be1, L0_gnn_ge, L0_gnn_bge, L0_gnn_We2, L0_gnn_be2, L0_gnn_Wn1, L0_gnn_bn1, L0_gnn_gn, L0_gnn_bgn, L0_gnn_Wn2, L0_gnn_bn2)
    return x

_drawn_inputs = setup_inputs


def setup_inputs(seed=0):
    import zlib

    import numpy as np

    out = dict(_drawn_inputs(seed))
    spreads = {'L0_gnn_be1': (0.0, 0.1),
     'L0_gnn_ge': (1.0, 0.2),
     'L0_gnn_bge': (0.0, 0.1),
     'L0_gnn_be2': (0.0, 0.1),
     'L0_gnn_bn1': (0.0, 0.1),
     'L0_gnn_gn': (1.0, 0.2),
     'L0_gnn_bgn': (0.0, 0.1),
     'L0_gnn_bn2': (0.0, 0.1)}
    factors = {}
    for name, (base, spread) in spreads.items():
        noise = np.random.default_rng([zlib.crc32(name.encode()), seed]).standard_normal(out[name].shape)
        drawn = base * np.exp(spread * noise) if base else spread * noise
        out[name] = jnp.asarray(drawn.astype(out[name].dtype))
    for name, factor in factors.items():
        out[name] = (out[name] * factor).astype(out[name].dtype)
    return out
```

```python
from contextlib import ExitStack

import numpy as np

import concourse.bass as bass
from concourse import mybir

F32 = mybir.dt.float32
F32R = mybir.dt.float32r
I32 = mybir.dt.int32
ALU = mybir.AluOpType
ACT = mybir.ActivationFunctionType
AXX = mybir.AxisListType.X

B, N, D = 128, 64, 128
PAIRS = B // 2
EPS = 1e-5
UNITS = 8
TILES = 8
K_B, K_A, K_S, K_E = 0, 64, 96, 112
K_ROWS = 114
SLOT = 48
W_LAG = 5
GELU_RING = 8
RING = 4
FIRST, LAST = 4, 60
RSQRT_MAGIC = 0x5F3759DF


class Pair:

    def __init__(self, c, turn=0, looped=False):
        self.c, self.turn, self.looped = c, turn, looped

    def __add__(self, d):
        return Pair(self.c + d, self.turn, self.looped)

    def __sub__(self, d):
        return self + (-d)

    def exists(self):
        return self.looped or 0 <= self.c < PAIRS

    def number(self):
        return self.turn * RING + self.c

    def ring(self, n):
        return self.c % n

    def count(self, each=1):
        return self.turn * (RING * each) + (self.c + 1) * each

    def count2(self, each):
        return self.turn * (RING // 2 * each) + (self.c // 2 + 1) * each

    def count4(self, each):
        return self.turn * each + (self.c // 4 + 1) * each

    def unit_count(self, u):
        return self.turn * (RING * UNITS) + self.c * UNITS + u + 1


def schedule(engine, iteration):
    for c in range(FIRST):
        iteration(Pair(c))
    with engine.Fori(0, (LAST - FIRST) // RING) as turn:
        for c in range(RING):
            iteration(Pair(FIRST + c, turn, True))
    for c in range(LAST, PAIRS + 2):
        iteration(Pair(c))


def build(nc, x, adj, We1, be1, ge, bge, We2, be2, Wn1, bn1, gn, bgn, Wn2, bn2, out):
    ctx = ExitStack()
    with ctx:
        def sb(name, shape, dt=F32):
            return ctx.enter_context(nc.sbuf_tensor(name, shape, dt))

        def pb(name, shape):
            return ctx.enter_context(nc.psum_tensor(name, shape, F32))

        def sem(name):
            return ctx.enter_context(nc.semaphore(name))

        def dram(name, shape):
            return nc.dram_tensor(name, shape, F32, kind="Internal").ap()

        store_a = dram("store_a", (PAIRS, 32, 2, 4, D))
        store_b = dram("store_b", (PAIRS, 64, 4, 2 * D))
        store_s = dram("store_s", (PAIRS, 4, 2, N, N))
        store_w = dram("store_w", (PAIRS, 4, 128, 32))

        ident = sb("ident", [128, 128])
        w1 = sb("w1", [128, 2, D])
        wn1 = sb("wn1", [128, 2, D])
        we2 = sb("we2", [128, D])
        we2T = sb("we2T", [128, D])
        wn2 = sb("wn2", [128, D])
        rows = sb("rows", [128, 5, D])
        be1_r, ge_r, bge_r, bn1_r, bn2_r = (rows[:, n, :] for n in range(5))
        cols = sb("cols", [128, 4])
        mean = sb("mean", [128, 3])
        w1c = sb("w1c", [128, 2, D])
        w_ah = sb("w_ah", [128, 2, D])
        w_b = sb("w_b", [128, D])
        be1c_col = sb("be1c_col", [128, 1])
        be1c_r = sb("be1c_r", [128, D])
        bias_hl = sb("bias_hl", [128, 4, D], F32R)
        rowmask = sb("rowmask", [128, 4, 4])
        gconst = sb("gconst", [128, 4, D])
        gtmp = sb("gtmp", [128, 4, D])
        be2_bc = sb("be2_bc", [128, 128])
        wc = sb("wc", [128, D])
        v_r = sb("v_r", [128, D])
        ones_a = sb("ones_a", [128, N])
        ones_b = sb("ones_b", [128, N])
        ones = sb("ones", [128, N])
        three_halves = sb("three_halves", [128, N])
        eps = sb("eps", [128, 1])
        offdiag = sb("offdiag", [128, N])
        pmask = sb("pmask", [128, 4])
        lstage = sb("lstage", [128, 16 * N])

        xin = sb("xin", [128, RING, D])
        adjin = sb("adjin", [128, 2, N])
        xT = sb("xT", [128, 128])
        a_hl = sb("a_hl", [128, 2, D], F32R)
        b_hl = sb("b_hl", [128, 2, 2, D], F32R)
        abT = sb("abT", [128, 2, 128])
        sq = sb("sq", [128, 2, 128])
        ve = sb("ve", [128, N])
        vh = sb("vh", [128, N])
        y = sb("y", [128, N])
        nt = sb("nt", [128, 2, N])
        std = sb("std", [128, N])
        s_hl = sb("s_hl", [128, 4, N], F32R)
        rw = sb("rw", [128, 32, 2, 2])
        rwT = sb("rwT", [128, 4, 32])
        sumw = sb("sumw", [128, 2])
        hx = sb("hx", [128, 2, D])
        vw = sb("vw", [128, D])
        hx2 = sb("hx2", [128, RING, D])
        xb = sb("xb", [128, RING, D])

        gmov = [sb(f"gmov{n}", [128, 4, 4 * D], F32R) for n in range(2)]
        lsta = [sb(f"lsta{n}", [128, 2, 16 * N], F32R) for n in range(2)]
        rwa = [sb(f"rwa{n}", [128, 4, 32]) for n in range(2)]
        wsel = [sb(f"wsel{n}", [128, UNITS * TILES, SLOT]) for n in range(2)]
        z = sb("z", [128, GELU_RING, TILES, D])
        g = sb("g", [128, GELU_RING, TILES, D])

        ms = sb("ms", [128, D])
        mT = sb("mT", [128, 128])
        hpre = sb("hpre", [128, D])
        stats = sb("stats", [128, 6])
        mv = sb("mv", [128, 2])
        vpe = sb("vpe", [128, 1])
        minus_half = sb("minus_half", [128, 1])
        rstd = sb("rstd", [128, 1])
        n1 = sb("n1", [128, D])
        g2T = sb("g2T", [128, 128])
        outs = sb("outs", [128, 2, D])

        up = [pb(f"up{n}", [128, TILES, D]) for n in range(2)]
        msg = [pb(f"msg{n}", [128, 512]) for n in range(2)]
        p0 = pb("p0", [128, 512])
        p1 = pb("p1", [128, 512])

        weights_in = sem("weights_in")
        pool_const = sem("pool_const")
        dve_const = sem("dve_const")
        we2T_full = sem("we2T_full")
        we2T_done = sem("we2T_done")
        fold_full = sem("fold_full")
        x_in = [sem(f"x_in{n}") for n in range(RING)]
        adj_in = [sem(f"adj_in{n}") for n in range(2)]
        ab_stored = sem("ab_stored")
        s_stored = sem("s_stored")
        w_stored = sem("w_stored")
        g_in = [sem(f"g_in{n}") for n in range(2)]
        l_in = [sem(f"l_in{n}") for n in range(2)]
        rwa_in = [sem(f"rwa_in{n}") for n in range(2)]
        out_stored = [sem(f"out_stored{n}") for n in range(2)]
        xT_full, xT_done = sem("xT_full"), sem("xT_done")
        ab_full, hi_done, lo_done = sem("ab_full"), sem("hi_done"), sem("lo_done")
        abT_full, abT_done, sq_done = sem("abT_full"), sem("abT_done"), sem("sq_done")
        v_full, ve_done, y_done = sem("v_full"), sem("ve_done"), sem("y_done")
        r_done, s_done, w_done = sem("r_done"), sem("s_done"), sem("w_done")
        rw_full, rwT_done = sem("rw_full"), sem("rwT_done")
        hx2_done, xb_done, wsel_done = sem("hx2_done"), sem("xb_done"), sem("wsel_done")
        u_full, z_done, g_done, sum_done = sem("u_full"), sem("z_done"), sem("g_done"), sem("sum_done")
        ms_done, mT_full, mT_done = sem("ms_done"), sem("mT_full"), sem("mT_done")
        h_full, h_read, mv_done, rstd_done = sem("h_full"), sem("h_read"), sem("mv_done"), sem("rstd_done")
        n1_done, n1T_full, g2_done = sem("n1_done"), sem("n1T_full"), sem("g2_done")
        y_full, out_done = sem("y_full"), sem("out_done")
        s_hi = sem("s_hi")
        dve_step, pool_step = sem("dve_step"), sem("pool_step")
        dve_stats, pool_newton, pool_hx, pool_rstd = (
            sem("dve_stats"), sem("pool_newton"), sem("pool_hx"), sem("pool_rstd"))

        x_v = x.rearrange("(k par) i f -> k (par i) f", par=2)
        adj_v = adj.rearrange("(k par) i j -> k (par i) j", par=2)
        out_v = out.rearrange("(k par) i f -> k (par i) f", par=2)

        def at(view, k):
            if not k.looped:
                return view[k.c]
            v = view[bass.ds(k.number(), 1)]
            names = " ".join("abcdef"[: len(view.shape) - 1])
            return v.rearrange(f"z {names} -> (z {names.split()[0]}) {' '.join(names.split()[1:])}")

        def row(v):
            return v.unsqueeze(0).to_broadcast([128, D])

        def col(v):
            return v.rearrange("(p o) -> p o", o=1)

        N_WEIGHTS = 15
        block = ctx.enter_context(nc.Block())

        @block.sync
        def _(sp):
            def load_x(k):
                if k.looped or k.c >= RING:
                    sp.wait_ge(xb_done, (k - RING).count())
                sp.dma_start(xin[:, k.ring(RING), :], at(x_v, k)).then_inc(x_in[k.ring(RING)], 16)

            def load_adj(k):
                if k.looped or k.c >= 2:
                    sp.wait_ge(w_done, (k - 2).count())
                sp.dma_start(adjin[:, k.ring(2), :], at(adj_v, k)).then_inc(adj_in[k.ring(2)], 16)

            def load_g(k):
                if k.looped or k.c >= 2:
                    sp.wait_ge(z_done, (k - 2).unit_count(UNITS - 1))
                if not k.looped:
                    sp.wait_ge(dve_const, 3)
                    sp.wait_ge(ab_stored, k.count(64))
                gv = gmov[k.ring(2)][:].bitcast(F32)
                for half in range(2):
                    sp.dma_start(gv[K_B:K_A, :, 2 * half * D:2 * (half + 1) * D],
                                 at(store_b, k)).then_inc(g_in[k.ring(2)], 16)
                src = at(store_a, k).rearrange("q par tl f -> q (par tl f)").unsqueeze(1)
                sp.dma_start(gv[K_A:K_S].rearrange("q (h par) x -> q h (par x)", h=2),
                             src.to_broadcast([32, 2, 2 * 4 * D])).then_inc(g_in[k.ring(2)], 16)

            def load_s(k):
                sp.wait_ge(s_stored, k.count(16))
                lv = lsta[k.ring(2)][:].bitcast(F32)
                sv = at(store_s, k)
                for par in range(2):
                    sp.dma_start(lv[K_S:K_E, par],
                                 sv[:, par].rearrange("c (tl r) j -> c tl (r j)", tl=4)).then_inc(l_in[k.ring(2)], 16)

            def store_rw(k):
                sp.wait_ge(rwT_done, k.count())
                sp.dma_start(at(store_w, k).rearrange("p q e -> q p e"), rwT[:]).then_inc(w_stored, 16)

            def load_rw(k):
                if not k.looped and k.c >= 2:
                    sp.wait_ge(wsel_done, (k - 2).count())
                sp.wait_ge(w_stored, k.count(16))
                sp.dma_start(rwa[k.ring(2)][:].rearrange("q a e -> q (a e)"),
                             at(store_w, k).rearrange("p (jl a) e -> (p jl) (a e)", a=4)).then_inc(rwa_in[k.ring(2)], 16)

            def store_ab(k):
                sp.wait_ge(lo_done, k.count())
                for hl in range(2):
                    dst = at(store_a, k)[16 * hl:16 * hl + 16].rearrange("r par tl f -> (par tl) r f")
                    sp.dma_start(dst, a_hl[:, hl, :].bitcast(F32)).then_inc(ab_stored, 16)
                    dst = at(store_b, k)[32 * hl:32 * hl + 32].rearrange("jl hp f -> hp jl f")
                    sp.dma_start(dst, b_hl[:, hl].bitcast(F32).rearrange("q r f -> q (r f)")).then_inc(ab_stored, 16)

            def store_std(k):
                sp.wait_ge(s_done, k.count())
                sp.dma_start(at(store_s, k).rearrange("c par i j -> (par i) c j"),
                             s_hl[:].bitcast(F32)).then_inc(s_stored, 16)

            def store_out(k):
                sp.wait_ge(out_done, k.count())
                sp.dma_start(at(out_v, k), outs[:, k.ring(2), :]).then_inc(out_stored[k.ring(2)], 16)

            for dst, src in ((w1[:, 0], We1[0:D]), (w1[:, 1], We1[D:2 * D]), (wn1[:, 0], Wn1[0:D]),
                             (wn1[:, 1], Wn1[D:2 * D]), (we2[:], We2), (wn2[:], Wn2),
                             (be1_r, row(be1)), (ge_r, row(ge)), (bge_r, row(bge)), (bn1_r, row(bn1)),
                             (bn2_r, row(bn2)), (cols[:, 0:1], col(be1)), (cols[:, 1:2], col(gn)),
                             (cols[:, 2:3], col(bgn)), (cols[:, 3:4], col(be2))):
                sp.dma_start(dst, src).then_inc(weights_in, 16)
            for c in range(RING):
                load_x(Pair(c))
            load_adj(Pair(0))
            load_adj(Pair(1))
            store_ab(Pair(0))
            store_std(Pair(0))
            load_g(Pair(0))
            load_s(Pair(0))
            store_rw(Pair(0))
            load_rw(Pair(0))
            load_adj(Pair(2))
            store_ab(Pair(1))
            store_std(Pair(1))
            store_ab(Pair(2))

            def iteration(k):
                if (k + 1).exists():
                    load_g(k + 1)
                    load_s(k + 1)
                if (k + 4).exists():
                    load_x(k + 4)
                if (k + 3).exists():
                    load_adj(k + 3)
                if (k + 1).exists():
                    store_rw(k + 1)
                    load_rw(k + 1)
                if (k + 3).exists():
                    store_ab(k + 3)
                if (k + 2).exists():
                    store_std(k + 2)
                if (k - 2).exists():
                    store_out(k - 2)

            schedule(sp, iteration)
            for n in range(2):
                sp.wait_ge(out_stored[n], PAIRS // 2 * 16)

        @block.gpsimd
        def _(pool):
            steps = [0]

            def link(ins):
                steps[0] += 1
                ins.then_inc(pool_step, 1)
                pool.wait_ge(pool_step, steps[0])

            def select(view, base, pattern):
                link(nc.gpsimd.affine_select(out=view, in_=view, compare_op=ALU.not_equal, fill=1.0,
                                             base=base, pattern=pattern, channel_multiplier=1))

            link(nc.gpsimd.memset(ident[:], 0.0))
            select(ident[:], 0, [[-1, 128]])
            link(nc.gpsimd.memset(ones_a[:], 1.0 / D))
            link(nc.gpsimd.memset(ones_b[:], 64.0 * 64.0 / D))
            link(nc.gpsimd.memset(ones[:], 1.0))
            link(nc.gpsimd.memset(three_halves[:], 1.5))
            link(nc.gpsimd.memset(eps[:], EPS))
            link(nc.gpsimd.memset(minus_half[:], -0.5))
            link(nc.gpsimd.memset(offdiag[:], 1.0))
            for par in range(2):
                v = offdiag[64 * par:64 * par + 64, :]
                link(nc.gpsimd.affine_select(out=v, in_=v, compare_op=ALU.not_equal, fill=0.0, base=0,
                                             pattern=[[-1, N]], channel_multiplier=1))
            nc.gpsimd.memset(pmask[:], 0.0).then_inc(pool_const, 1)
            link(nc.gpsimd.memset(lstage[:], 0.0))
            link(nc.gpsimd.memset(lstage[96:128, :], 1.0))
            for first in (0, 32):
                select(lstage[first:first + 32, :].rearrange("q (r jl h) -> q r jl h", jl=32, h=2), 0,
                       [[0, 16], [-1, 32], [0, 2]])
            for base in (0, -16):
                select(lstage[64:96, :].rearrange("q (r j) -> q r j", j=N), base, [[-1, 16], [0, N]])
            link(nc.gpsimd.memset(rowmask[:], 0.0))
            for m, offs in ((0, (0, 8)), (1, (4, 12))):
                for off in offs:
                    select(rowmask[96:128, m, :], -off, [[-1, 4]])
            for m, off in ((2, 16), (3, 17)):
                select(rowmask[96:128, m, :], -off, [[0, 4]])
            nc.gpsimd.memset(gtmp[:], 0.0).then_inc(pool_const, 1)
            pool.wait_ge(pool_const, 2)
            for p in range(4):
                link(nc.gpsimd.memset(pmask[32 * p:32 * p + 32, p:p + 1], 1.0))

            def squares(k):
                pool.wait_ge(abT_done, k.count())
                if (k - 1).exists():
                    pool.wait_ge(v_full, (k - 1).count())
                nc.gpsimd.tensor_tensor(sq[:], abT[:], abT[:], ALU.mult).then_inc(sq_done, 1)

            def newton(k):
                pool.wait_ge(y_done, k.count())
                done = 0

                def step(ins):
                    nonlocal done
                    done += 1
                    ins.then_inc(pool_newton, 1)
                    pool.wait_ge(pool_newton, (k - 1).count(13) + done)

                for it in range(3):
                    step(nc.gpsimd.tensor_tensor(nt[:, 0], y[:], y[:], ALU.mult))
                    step(nc.gpsimd.tensor_tensor(nt[:, 1], nt[:, 0], vh[:], ALU.mult))
                    step(nc.gpsimd.tensor_tensor(nt[:, 0], nt[:, 1], three_halves[:], ALU.add))
                    step(nc.gpsimd.tensor_tensor(y[:], y[:], nt[:, 0], ALU.mult))
                if (k - 1).exists():
                    pool.wait_ge(rw_full, (k - 1).count())
                    pool.wait_ge(s_stored, (k - 1).count(16))
                nc.gpsimd.tensor_tensor(rw[:, :, 0, :], y[:].rearrange("q (jl h) -> q jl h", h=2),
                                        ones[:].rearrange("q (jl h) -> q jl h", h=2), ALU.mult).then_inc(r_done, 1)
                nc.gpsimd.tensor_tensor(std[:], ve[:], y[:], ALU.mult).then_inc(pool_newton, 1)
                twice = std[:].unsqueeze(1).to_broadcast([128, 2, N])
                nc.gpsimd.tensor_tensor(s_hl[:, 0:2], ve[:].unsqueeze(1).to_broadcast([128, 2, N]),
                                        y[:].unsqueeze(1).to_broadcast([128, 2, N]), ALU.mult).then_inc(s_hi, 1)
                pool.wait_ge(pool_newton, k.count(13))
                pool.wait_ge(s_hi, k.count())
                nc.gpsimd.tensor_tensor(s_hl[:, 2:4], twice, s_hl[:, 0:2].bitcast(F32),
                                        ALU.subtract).then_inc(s_done, 1)

            def node_bias(k):
                pool.wait_ge(hi_done, k.count())
                pool.wait_ge(w_done, k.count())
                nc.gpsimd.tensor_tensor(vw[:], v_r[:], sumw[:, k.ring(2):k.ring(2) + 1].to_broadcast([128, D]),
                                        ALU.mult).then_inc(pool_hx, 1)
                pool.wait_ge(pool_hx, (k - 1).count(2) + 1)
                nc.gpsimd.tensor_tensor(vw[:], vw[:], bn1_r, ALU.add).then_inc(pool_hx, 1)
                pool.wait_ge(pool_hx, k.count(2))
                if (k - RING).exists() or k.looped:
                    pool.wait_ge(h_read, (k - RING).count())
                nc.gpsimd.tensor_tensor(hx2[:, k.ring(RING), :], hx[:, k.ring(2), :], vw[:],
                                        ALU.add).then_inc(hx2_done, 1)

            def select_weights(k):
                pool.wait_ge(rwa_in[k.ring(2)], k.count2(16))
                if (k - 2).exists() or k.looped:
                    pool.wait_ge(sum_done, (k - 2).unit_count(UNITS - 1))
                w = rwa[k.ring(2)][:, 2:4, :].rearrange("q h e -> q (h e)")
                nc.gpsimd.tensor_tensor(wsel[k.ring(2)][:, :, 0:4],
                                        w.unsqueeze(2).to_broadcast([128, UNITS * TILES, 4]),
                                        pmask[:].unsqueeze(1).to_broadcast([128, UNITS * TILES, 4]),
                                        ALU.mult).then_inc(wsel_done, 1)

            def residual(k):
                pool.wait_ge(x_in[k.ring(RING)], k.count4(16))
                pool.wait_ge(xT_full, k.count())
                if (k - RING).exists() or k.looped:
                    pool.wait_ge(out_done, (k - RING).count())
                nc.gpsimd.tensor_tensor(xb[:, k.ring(RING), :], xin[:, k.ring(RING), :], bn2_r,
                                        ALU.add).then_inc(xb_done, 1)

            def node_rstd(k):
                pool.wait_ge(mv_done, k.count())
                nc.gpsimd.tensor_tensor(vpe[:], mv[:, 1:2], eps[:], ALU.add).then_inc(pool_rstd, 1)
                pool.wait_ge(pool_rstd, k.count())
                if (k - 1).exists():
                    pool.wait_ge(n1_done, (k - 1).count())
                nc.gpsimd.tensor_tensor(rstd[:], vpe[:], minus_half[:], ALU.pow).then_inc(rstd_done, 1)

            pool.wait_ge(weights_in, 16 * N_WEIGHTS)
            pool.wait_ge(dve_const, 2)
            squares(Pair(0))
            newton(Pair(0))
            node_bias(Pair(0))
            residual(Pair(0))
            squares(Pair(1))
            newton(Pair(1))
            node_bias(Pair(1))
            residual(Pair(1))
            squares(Pair(2))
            pool.wait_ge(dve_const, 3)
            select_weights(Pair(0))

            def iteration(k):
                if (k - 2).exists():
                    node_rstd(k - 2)
                if (k + 2).exists():
                    newton(k + 2)
                if (k + 2).exists():
                    residual(k + 2)
                if (k + 3).exists():
                    squares(k + 3)
                if (k + 1).exists():
                    select_weights(k + 1)
                if (k + 2).exists():
                    node_bias(k + 2)

            schedule(pool, iteration)

        @block.scalar
        def _(act):
            def copy_xT(k):
                act.wait_ge(xT_full, k.count())
                if (k - 1).exists():
                    act.wait_ge(ab_full, (k - 1).count())
                    act.wait_ge(abT_full, (k - 1).count())
                nc.scalar.copy(xT[:], p1[:, 0:128]).then_inc(xT_done, 1)

            def high_parts(k):
                act.wait_ge(ab_full, k.count())
                if (k - 1).exists():
                    act.wait_ge(ab_stored, (k - 1).count(64))
                if (k - 2).exists() or k.looped:
                    act.wait_ge(hx2_done, (k - 2).count())
                nc.scalar.copy(a_hl[:, 0], p0[:, 0:D])
                nc.scalar.copy(hx[:, k.ring(2), :], p0[:, D:2 * D])
                nc.scalar.copy(b_hl[:, 0], p0[:, 2 * D:3 * D].unsqueeze(1).to_broadcast([128, 2, D])).then_inc(hi_done, 1)

            def copy_abT(k):
                act.wait_ge(abT_full, k.count())
                if (k - 1).exists():
                    act.wait_ge(v_full, (k - 1).count())
                    act.wait_ge(sq_done, (k - 1).count())
                nc.scalar.activation(abT[:, 0], p1[:, 0:128], ACT.Identity, bias=be1c_col[:])
                nc.scalar.copy(abT[:, 1], p1[:, 128:256]).then_inc(abT_done, 1)

            def copy_rwT(k):
                act.wait_ge(rw_full, k.count())
                if (k - 1).exists():
                    act.wait_ge(w_stored, (k - 1).count(16))
                src = p1[:, 0:128].rearrange("q (pt tq p) -> q p tq pt", pt=8, tq=4)
                nc.scalar.copy(rwT[:].rearrange("q p (tq pt) -> q p tq pt", tq=4), src).then_inc(rwT_done, 1)

            def copy_messages(k):
                act.wait_ge(sum_done, k.unit_count(UNITS - 1))
                if (k - 1).exists():
                    act.wait_ge(mT_full, (k - 1).count())
                nc.scalar.copy(ms[:], msg[k.ring(2)][:, 0:D]).then_inc(ms_done, 1)

            def copy_mT(k):
                act.wait_ge(mT_full, k.count())
                if (k - 1).exists():
                    act.wait_ge(h_full, (k - 1).count())
                nc.scalar.copy(mT[:], p1[:, 0:128]).then_inc(mT_done, 1)

            def node_gelu(k):
                act.wait_ge(n1T_full, k.count())
                if (k - 1).exists():
                    act.wait_ge(y_full, (k - 1).count())
                nc.scalar.activation(g2T[:], p1[:, 0:128], ACT.Gelu, bias=cols[:, 2:3],
                                     scale=cols[:, 1:2]).then_inc(g2_done, 1)

            def edge_gelu(k, u):
                act.wait_ge(z_done, k.unit_count(u))
                if k.looped or k.c * UNITS + u >= GELU_RING:
                    act.wait_ge(sum_done, k.unit_count(u - GELU_RING))
                nc.scalar.activation(g[:, u % GELU_RING], z[:, u % GELU_RING], ACT.Gelu).then_inc(g_done, 1)

            act.wait_ge(weights_in, 16 * N_WEIGHTS)
            act.wait_ge(we2T_full, 1)
            nc.scalar.copy(we2T[:], p1[:, 0:128]).then_inc(we2T_done, 1)
            act.wait_ge(dve_const, 2)
            for c in range(3):
                copy_xT(Pair(c))
                high_parts(Pair(c))
                copy_abT(Pair(c))
                if c == 0:
                    copy_rwT(Pair(0))

            def iteration(k):
                for u in range(UNITS):
                    if k.exists():
                        edge_gelu(k, u)
                    if u == 1 and (k + 1).exists():
                        copy_rwT(k + 1)
                    if u == 1 and (k + 3).exists():
                        copy_xT(k + 3)
                    if u == 2 and (k - 1).exists():
                        copy_messages(k - 1)
                    if u == 3 and (k + 3).exists():
                        high_parts(k + 3)
                    if u == 3 and (k - 2).exists():
                        node_gelu(k - 2)
                    if u == 3 and (k - 1).exists():
                        copy_mT(k - 1)
                    if u == 6 and (k + 3).exists():
                        copy_abT(k + 3)

            schedule(act, iteration)

        @block.vector
        def _(dve):
            steps = [0]

            def link(ins):
                steps[0] += 1
                ins.then_inc(dve_step, 1)
                dve.wait_ge(dve_step, steps[0])

            def low_parts(k):
                dve.wait_ge(hi_done, k.count())
                nc.vector.tensor_tensor(a_hl[:, 1], p0[:, 0:D], a_hl[:, 0].bitcast(F32), ALU.subtract)
                nc.vector.tensor_tensor(b_hl[:, 1], p0[:, 2 * D:3 * D].unsqueeze(1).to_broadcast([128, 2, D]),
                                        b_hl[:, 0].bitcast(F32), ALU.subtract).then_inc(lo_done, 1)

            def weights(k):
                dve.wait_ge(adj_in[k.ring(2)], k.count2(16))
                if (k - 1).exists():
                    dve.wait_ge(rw_full, (k - 1).count())
                if (k - 2).exists() or k.looped:
                    dve.wait_ge(hx2_done, (k - 2).count())
                nc.vector.scalar_tensor_tensor(
                    out=rw[:, :, 1, :], in0=adjin[:, k.ring(2), :].rearrange("q (jl h) -> q jl h", h=2), scalar=1.0,
                    in1=offdiag[:].rearrange("q (jl h) -> q jl h", h=2), op0=ALU.mult, op1=ALU.mult,
                    accum_out=sumw[:, k.ring(2):k.ring(2) + 1]).then_inc(w_done, 1)

            def variance(k):
                dve.wait_ge(v_full, k.count())
                if (k - 1).exists():
                    dve.wait_ge(s_done, (k - 1).count())
                nc.vector.tensor_scalar(ve[:], p0[:, 0:N], 0.0, EPS, ALU.max, ALU.add).then_inc(ve_done, 1)

            def first_guess(k):
                dve.wait_ge(ve_done, k.count())
                nc.vector.tensor_scalar(vh[:], ve[:], -0.5, None, ALU.mult)
                nc.vector.tensor_scalar(y[:].bitcast(I32), ve[:].bitcast(I32), -0.5, float(RSQRT_MAGIC), ALU.mult,
                                        ALU.add).then_inc(y_done, 1)

            def node_sum(k):
                dve.wait_ge(h_full, k.count())
                dve.wait_ge(hx2_done, k.count())
                nc.vector.tensor_tensor(hpre[:], p0[:, 0:D], hx2[:, k.ring(RING), :], ALU.add).then_inc(h_read, 1)

            def node_stats(k):
                dve.wait_ge(h_read, k.count())
                nc.vector.bn_stats(stats[:], hpre[:]).then_inc(dve_stats, 1)

            def weights_and_mean(k_w, k):
                if k.exists():
                    dve.wait_ge(dve_stats, k.count())
                    if (k - 1).exists():
                        dve.wait_ge(rstd_done, (k - 1).count())
                if k_w.exists():
                    weights(k_w)
                if k.exists():
                    nc.vector.bn_aggr(mv[:], stats[:]).then_inc(mv_done, 1)

            def normalise(k):
                dve.wait_ge(rstd_done, k.count())
                if (k - 1).exists():
                    dve.wait_ge(n1T_full, (k - 1).count())
                nc.vector.tensor_scalar(n1[:], hpre[:], mv[:, 0:1], rstd[:], ALU.subtract,
                                        ALU.mult).then_inc(n1_done, 1)

            def finish(k):
                dve.wait_ge(y_full, k.count())
                dve.wait_ge(xb_done, k.count())
                if (k - 2).exists() or k.looped:
                    dve.wait_ge(out_stored[k.ring(2)], (k - 2).count2(16))
                nc.vector.tensor_tensor(outs[:, k.ring(2), :], p0[:, 0:D], xb[:, k.ring(RING), :],
                                        ALU.add).then_inc(out_done, 1)

            def scale(k, u):
                dve.wait_ge(u_full, k.unit_count(u))
                if u == 0:
                    dve.wait_ge(rwa_in[k.ring(2)], k.count2(16))
                if k.looped or k.c * UNITS + u >= GELU_RING:
                    dve.wait_ge(g_done, k.unit_count(u - GELU_RING))
                h, tq = divmod(u, 4)
                r = rwa[k.ring(2)][:, h, TILES * tq:TILES * (tq + 1)]
                nc.vector.tensor_tensor(z[:, u % GELU_RING], up[u % 2][:],
                                        r.unsqueeze(2).to_broadcast([128, TILES, D]), ALU.mult).then_inc(z_done, 1)

            dve.wait_ge(weights_in, 16 * N_WEIGHTS)
            link(nc.vector.reduce_sum(mean[:, 0:2], w1[:], axis=AXX))
            link(nc.vector.reduce_sum(mean[:, 2:3], be1_r, axis=AXX))
            link(nc.vector.tensor_scalar(mean[:], mean[:], 1.0 / D, None, ALU.mult))
            link(nc.vector.tensor_scalar(w1c[:, 0], w1[:, 0], mean[:, 0:1], None, ALU.subtract))
            link(nc.vector.tensor_scalar(w1[:, 1], w1[:, 1], mean[:, 1:2], None, ALU.subtract))
            link(nc.vector.tensor_scalar(w1c[:, 1], w1[:, 1], 1.0 / 64, None, ALU.mult))
            link(nc.vector.tensor_tensor(w_ah[:, 0], w1c[:, 0], ge_r, ALU.mult))
            link(nc.vector.tensor_copy(w_ah[:, 1], wn1[:, 0]))
            link(nc.vector.tensor_tensor(w_b[:], w1[:, 1], ge_r, ALU.mult))
            link(nc.vector.tensor_scalar(be1c_r[:], be1_r, mean[:, 2:3], None, ALU.subtract))
            link(nc.vector.tensor_scalar(be1c_col[:], cols[:, 0:1], mean[:, 2:3], None, ALU.subtract))
            link(nc.vector.tensor_tensor(be1c_r[:], be1c_r[:], ge_r, ALU.mult))
            link(nc.vector.tensor_copy(be2_bc[:], cols[:, 3:4].to_broadcast([128, 128])))
            for m, src in ((0, bge_r), (2, be1c_r[:])):
                link(nc.vector.tensor_copy(bias_hl[:, m], src))
                link(nc.vector.tensor_tensor(bias_hl[:, m + 1], src, bias_hl[:, m].bitcast(F32), ALU.subtract))
            nc.vector.memset(sumw[:], 0.0).then_inc(dve_const, 1)
            dve.wait_ge(fold_full, 1)
            nc.vector.tensor_copy(wc[:], p0[:, 0:D])
            nc.vector.tensor_copy(v_r[:], p0[:, D:2 * D]).then_inc(dve_const, 1)
            dve.wait_ge(pool_const, 1)
            weights(Pair(0))
            low_parts(Pair(0))
            variance(Pair(0))
            first_guess(Pair(0))
            dve.wait_ge(pool_const, 2)
            q = slice(K_S, 128)
            for m in range(4):
                dst = gconst if m == 0 else gtmp
                link(nc.vector.tensor_tensor(dst[q], bias_hl[q, m].bitcast(F32).unsqueeze(1).to_broadcast([32, 4, D]),
                                             rowmask[q, m].unsqueeze(2).to_broadcast([32, 4, D]), ALU.mult))
                if m:
                    link(nc.vector.tensor_tensor(gconst[q], gconst[q], gtmp[q], ALU.add))
            for n in range(2):
                for par in range(2):
                    nc.vector.tensor_copy(lsta[n][:, par], lstage[:])
                link(nc.vector.tensor_copy(
                    gmov[n][q], gconst[q].rearrange("q t f -> q (t f)").unsqueeze(1).to_broadcast([32, 4, 4 * D])))
            nc.vector.memset(wsel[0][:], 0.0)
            nc.vector.memset(wsel[1][:], 0.0).then_inc(dve_const, 1)
            weights(Pair(1))
            low_parts(Pair(1))
            variance(Pair(1))
            first_guess(Pair(1))
            low_parts(Pair(2))

            def iteration(k):
                for u in range(UNITS):
                    if k.exists():
                        scale(k, u)
                    if u == 0 and (k - 2).exists():
                        node_sum(k - 2)
                    if u == 1 and (k - 2).exists():
                        node_stats(k - 2)
                    if u == 2 and (k + 2).exists():
                        variance(k + 2)
                    if u == 2:
                        weights_and_mean(k + 2, k - 2)
                    if u == 3 and (k + 2).exists():
                        first_guess(k + 2)
                    if u == 4 and (k - 2).exists():
                        normalise(k - 2)
                    if u == 5 and (k + 3).exists():
                        low_parts(k + 3)
                    if u == 7 and (k - 2).exists():
                        finish(k - 2)

            schedule(dve, iteration)

        @block.tensor
        def _(pe):
            def transpose_x(k, free=None):
                pe.wait_ge(x_in[k.ring(RING)], k.count4(16))
                if free:
                    pe.wait_ge(*free)
                nc.tensor.transpose(p1[:, 0:128], xin[:, k.ring(RING), :], ident[:]).then_inc(xT_full, 1)

            def node_products(k, free=None):
                pe.wait_ge(xT_done, k.count())
                if free:
                    pe.wait_ge(*free)
                nc.tensor.matmul(p0[:, 0:2 * D], xT[:], w_ah[:].rearrange("q a f -> q (a f)"), start=True, stop=True)
                by_h = xT[:].rearrange("q (m h) -> q h m", h=2)
                for h in range(2):
                    last = nc.tensor.matmul(p0[64 * h:64 * h + 64, 2 * D:3 * D], by_h[:, h], w_b[:],
                                            start=True, stop=True)
                last.then_inc(ab_full, 1)

            def feature_products(k, free=None):
                pe.wait_ge(xT_done, k.count())
                if free:
                    pe.wait_ge(*free)
                nc.tensor.matmul(p1[:, 0:128], w1c[:, 0], xT[:], start=True, stop=True)
                nc.tensor.matmul(p1[:, 128:256], w1c[:, 1], xT[:], start=True, stop=True).then_inc(abT_full, 1)

            def variances(k, free):
                pe.wait_ge(sq_done, k.count())
                pe.wait_ge(*free)
                terms = ((lambda s: abT[:, 0, s], lambda s: abT[:, 1, s]),
                         (lambda s: sq[:, 0, s], lambda s: ones_a[:]),
                         (lambda s: ones_b[:], lambda s: sq[:, 1, s]))
                for t, (left, right) in enumerate(terms):
                    for par in range(2):
                        s = slice(64 * par, 64 * par + 64)
                        last = nc.tensor.matmul(p0[s, 0:N], left(s), right(s), start=(t == 0), stop=(t == 2))
                last.then_inc(v_full, 1)

            def transpose_rw(k, free):
                pe.wait_ge(r_done, k.count())
                pe.wait_ge(w_done, k.count())
                if free:
                    pe.wait_ge(*free)
                nc.tensor.transpose(p1[:, 0:128], rw[:].rearrange("q jl a h -> q (jl a h)"), ident[:]).then_inc(rw_full, 1)

            def u_product(k, u):
                if u == 0:
                    pe.wait_ge(g_in[k.ring(2)], k.count2(48))
                    pe.wait_ge(l_in[k.ring(2)], k.count2(32))
                if k.looped or k.c * UNITS + u >= 2:
                    pe.wait_ge(z_done, k.unit_count(u - 2))
                h, tq = divmod(u, 4)
                for par in range(2):
                    selector = lsta[k.ring(2)][0:K_ROWS, par, 256 * tq:256 * tq + 256].rearrange("q (e h) -> q h e", h=2)
                    last = nc.tensor.matmul(up[u % 2][:, 4 * par:4 * par + 4, :].rearrange("q t f -> q (t f)"),
                                            selector[:, h],
                                            gmov[k.ring(2)][0:K_ROWS, 2 * h + par, :], start=True, stop=True)
                last.then_inc(u_full, 1)

            def weighted_sum(k, u):
                pe.wait_ge(g_done, k.unit_count(u))
                if u == 0:
                    pe.wait_ge(wsel_done, k.count())
                    if (k - 2).exists() or k.looped:
                        pe.wait_ge(ms_done, (k - 2).count())
                tq = u % 4
                ws = wsel[k.ring(2)][:].rearrange("q t s -> q (t s)")
                for tl0 in range(2):
                    for c in range(4):
                        tile = 4 * (c // 2) + 2 * (c % 2) + tl0
                        at0 = SLOT * (TILES * u + tile) - 16 * tl0 - 4 * tq
                        last = nc.tensor.matmul(msg[k.ring(2)][32 * c:32 * c + 32, 0:D], ws[:, at0:at0 + 32],
                                                g[:, u % GELU_RING, tile, :], start=(u == 0 and tl0 == 0),
                                                stop=(u == UNITS - 1 and tl0 == 1))
                last.then_inc(sum_done, 1)

            def transpose_messages(k, free):
                pe.wait_ge(ms_done, k.count())
                pe.wait_ge(*free)
                nc.tensor.transpose(p1[:, 0:128], ms[:], ident[:]).then_inc(mT_full, 1)

            def node_hidden(k, free):
                pe.wait_ge(mT_done, k.count())
                pe.wait_ge(*free)
                nc.tensor.matmul(p0[:, 0:D], mT[:], wc[:], start=True, stop=True).then_inc(h_full, 1)

            def transpose_n1(k, free):
                pe.wait_ge(n1_done, k.count())
                pe.wait_ge(*free)
                nc.tensor.transpose(p1[:, 0:128], n1[:], ident[:]).then_inc(n1T_full, 1)

            def node_output(k, free):
                pe.wait_ge(g2_done, k.count())
                pe.wait_ge(*free)
                nc.tensor.matmul(p0[:, 0:D], g2T[:], wn2[:], start=True, stop=True).then_inc(y_full, 1)

            pe.wait_ge(weights_in, 16 * N_WEIGHTS)
            pe.wait_ge(pool_const, 1)
            nc.tensor.transpose(p1[:, 0:128], we2[:], ident[:]).then_inc(we2T_full, 1)
            pe.wait_ge(we2T_done, 1)
            pe.wait_ge(dve_const, 1)
            nc.tensor.matmul(p0[:, 0:D], we2T[:], wn1[:, 1], start=True, stop=True)
            nc.tensor.matmul(p0[:, D:2 * D], be2_bc[:], wn1[:, 1], start=True, stop=True).then_inc(fold_full, 1)
            transpose_x(Pair(0), (we2T_done, 1))
            node_products(Pair(0), (dve_const, 2))
            feature_products(Pair(0))
            variances(Pair(0), (lo_done, 1))
            transpose_rw(Pair(0), (abT_done, 1))
            transpose_x(Pair(1), (rwT_done, 1))
            node_products(Pair(1), (ve_done, 1))
            feature_products(Pair(1))
            variances(Pair(1), (lo_done, 2))
            transpose_x(Pair(2), (abT_done, 2))
            node_products(Pair(2), (ve_done, 2))
            feature_products(Pair(2))

            def iteration(k):
                nxt, two, three, prev, old = (k + 1).exists(), (k + 2).exists(), (k + 3).exists(), k - 1, k - 2
                for u in range(UNITS):
                    if k.exists():
                        u_product(k, u)
                    w = u - W_LAG
                    if w >= 0 and k.exists():
                        weighted_sum(k, w)
                    if w < 0 and prev.exists():
                        weighted_sum(prev, w + UNITS)
                    if u == 0 and old.exists():
                        node_hidden(old, (out_done, (k - 3).count()) if (k - 3).exists()
                                         else (lo_done, (k + 2).count()))
                    if u == 1 and nxt:
                        transpose_rw(k + 1, (abT_done, (k + 2).count()) if two
                                            else (mT_done, old.count()))
                    if u == 2 and two:
                        variances(k + 2, (h_read, old.count()) if old.exists()
                                         else (lo_done, (k + 2).count()))
                    if u == 3 and three:
                        transpose_x(k + 3, (rwT_done, (k + 1).count()))
                    if u == 4 and three:
                        node_products(k + 3, (ve_done, (k + 2).count()))
                    if u == 5 and old.exists():
                        transpose_n1(old, (xT_done, (k + 3).count()) if three
                                          else (rwT_done, (k + 1).count()) if nxt
                                          else (mT_done, old.count()))
                    if u == 6 and prev.exists():
                        transpose_messages(prev, (g2_done, old.count()) if old.exists()
                                                 else (xT_done, (k + 3).count()))
                    if u == 7 and three:
                        feature_products(k + 3, (mT_done, prev.count()) if prev.exists()
                                                else (xT_done, (k + 3).count()))
                    if u == 7 and old.exists():
                        node_output(old, (lo_done, (k + 3).count()) if three
                                         else (ve_done, (k + 2).count()) if two
                                         else (h_read, old.count()))

            schedule(pe, iteration)


_WEIGHTS = ['We1', 'be1', 'ge', 'bge', 'We2', 'be2', 'Wn1', 'bn1', 'gn', 'bgn', 'Wn2', 'bn2']


def kernel(x, adj, **weights):
    import concourse.bacc as _bacc
    from concourse.bass_utils import run_bass_kernel_spmd as _run

    given = {"x": x, "adj": adj} | {name: weights[f"L0_gnn_{name}"] for name in _WEIGHTS}
    nc = _bacc.Bacc("TRN2", target_bir_lowering=False, num_devices=1)
    arrays, args = {}, []
    for name, a in given.items():
        a = np.ascontiguousarray(a)
        arrays[f"in_{name}"] = a
        args.append(nc.dram_tensor(f"in_{name}", a.shape, mybir.dt.from_np(a.dtype), kind="ExternalInput").ap())
    args.append(nc.dram_tensor("out_x", (B, N, D), F32, kind="ExternalOutput").ap())
    build(nc, *args)
    r = _run(nc, [arrays], core_ids=[0])
    return r.results[0]["out_x"]
```

```python
from contextlib import ExitStack

import numpy as np

import concourse.bass as bass
from concourse import mybir

F32 = mybir.dt.float32
F32R = mybir.dt.float32r
I32 = mybir.dt.int32
ALU = mybir.AluOpType
ACT = mybir.ActivationFunctionType
AXX = mybir.AxisListType.X

B, N, D = 128, 64, 128
PAIRS = B // 2
EPS = 1e-5
UNITS = 8
TILES = 8
K_B, K_A, K_S, K_E = 0, 64, 96, 112
K_ROWS = 114
SLOT = 48
W_LAG = 5
GELU_RING = 8
RING = 4
BODY = 8
FIRST, LAST = 4, 60
RSQRT_MAGIC = 0x5F3759DF


class Pair:

    def __init__(self, c, turn=0, looped=False):
        self.c, self.turn, self.looped = c, turn, looped

    def __add__(self, d):
        return Pair(self.c + d, self.turn, self.looped)

    def __sub__(self, d):
        return self + (-d)

    def exists(self):
        return self.looped or 0 <= self.c < PAIRS

    def number(self):
        return self.turn * BODY + self.c

    def ring(self, n):
        return self.c % n

    def count(self, each=1):
        return self.turn * (BODY * each) + (self.c + 1) * each

    def count2(self, each):
        return self.turn * (BODY // 2 * each) + (self.c // 2 + 1) * each

    def count4(self, each):
        return self.turn * (BODY // 4 * each) + (self.c // 4 + 1) * each

    def unit_count(self, u):
        return self.turn * (BODY * UNITS) + self.c * UNITS + u + 1


def schedule(engine, iteration):
    for c in range(FIRST):
        iteration(Pair(c))
    with engine.Fori(0, (LAST - FIRST) // BODY) as turn:
        for c in range(BODY):
            iteration(Pair(FIRST + c, turn, True))
    for c in range(LAST, PAIRS + 2):
        iteration(Pair(c))


def build(nc, x, adj, We1, be1, ge, bge, We2, be2, Wn1, bn1, gn, bgn, Wn2, bn2, out):
    ctx = ExitStack()
    with ctx:
        def sb(name, shape, dt=F32):
            return ctx.enter_context(nc.sbuf_tensor(name, shape, dt))

        def pb(name, shape):
            return ctx.enter_context(nc.psum_tensor(name, shape, F32))

        def sem(name):
            return ctx.enter_context(nc.semaphore(name))

        def dram(name, shape):
            return nc.dram_tensor(name, shape, F32, kind="Internal").ap()

        store_a = dram("store_a", (PAIRS, 32, 2, 4, D))
        store_b = dram("store_b", (PAIRS, 64, 4, 2 * D))
        store_s = dram("store_s", (PAIRS, 4, 2, N, N))
        store_w = dram("store_w", (PAIRS, 4, 128, 32))

        ident = sb("ident", [128, 128])
        w1 = sb("w1", [128, 2, D])
        wn1 = sb("wn1", [128, 2, D])
        we2 = sb("we2", [128, D])
        we2T = sb("we2T", [128, D])
        wn2 = sb("wn2", [128, D])
        rows = sb("rows", [128, 5, D])
        be1_r, ge_r, bge_r, bn1_r, bn2_r = (rows[:, n, :] for n in range(5))
        cols = sb("cols", [128, 4])
        mean = sb("mean", [128, 3])
        w1c = sb("w1c", [128, 2, D])
        w_ah = sb("w_ah", [128, 2, D])
        w_b = sb("w_b", [128, D])
        be1c_col = sb("be1c_col", [128, 1])
        be1c_r = sb("be1c_r", [128, D])
        bias_hl = sb("bias_hl", [128, 4, D], F32R)
        rowmask = sb("rowmask", [128, 4, 4])
        gconst = sb("gconst", [128, 4, D])
        grow = sb("grow", [128, 2, D])
        be2_bc = sb("be2_bc", [128, 128])
        wc = sb("wc", [128, D])
        v_r = sb("v_r", [128, D])
        ones_a = sb("ones_a", [128, N])
        ones_b = sb("ones_b", [128, N])
        ones = sb("ones", [128, N])
        three_halves = sb("three_halves", [128, N])
        halves = sb("halves", [128, N])
        eps = sb("eps", [128, 1])
        offdiag = sb("offdiag", [128, N])
        pmask = sb("pmask", [128, 4])
        sel = sb("sel", [128, 32])
        lstage = sb("lstage", [128, 16 * N])

        xin = sb("xin", [128, RING, D])
        adjin = sb("adjin", [128, 2, N])
        xT = sb("xT", [128, 128])
        a_hl = sb("a_hl", [128, 2, D], F32R)
        b_hl = sb("b_hl", [128, 2, 2, D], F32R)
        abT = sb("abT", [128, 2, 128])
        sq = sb("sq", [128, 2, 128])
        ve = sb("ve", [128, N])
        vh = sb("vh", [128, N])
        y = sb("y", [128, N])
        nt = sb("nt", [128, 2, N])
        std = sb("std", [128, N])
        s_hl = sb("s_hl", [128, 4, N], F32R)
        rw = sb("rw", [128, 32, 2, 2])
        rwT = sb("rwT", [128, 4, 32])
        sumw = sb("sumw", [128, 2])
        hx = sb("hx", [128, RING, D])
        vw = sb("vw", [128, 2, D])
        hx2 = sb("hx2", [128, RING, D])
        xb = sb("xb", [128, RING, D])

        gmov = [sb(f"gmov{n}", [128, 4, 4 * D], F32R) for n in range(2)]
        lsta = [sb(f"lsta{n}", [128, 2, 16 * N], F32R) for n in range(2)]
        rwa = [sb(f"rwa{n}", [128, 4, 32]) for n in range(2)]
        wsel = [sb(f"wsel{n}", [128, UNITS * TILES, SLOT]) for n in range(2)]
        z = sb("z", [128, GELU_RING, TILES, D])
        g = sb("g", [128, GELU_RING, TILES, D])

        ms = sb("ms", [128, D])
        mT = sb("mT", [128, 128])
        hpre = sb("hpre", [128, D])
        stats = sb("stats", [128, 6])
        mv = sb("mv", [128, 2])
        vpe = sb("vpe", [128, 1])
        minus_half = sb("minus_half", [128, 1])
        rstd = sb("rstd", [128, 1])
        n1 = sb("n1", [128, D])
        g2T = sb("g2T", [128, 128])
        outs = sb("outs", [128, 2, D])

        up = [pb(f"up{n}", [128, TILES, D]) for n in range(2)]
        msg = [pb(f"msg{n}", [128, 512]) for n in range(2)]
        p0 = pb("p0", [128, 512])
        p1 = pb("p1", [128, 512])

        first_in, weights_in = sem("first_in"), sem("weights_in")
        ident_done, pool_const = sem("ident_done"), sem("pool_const")
        lstage_done, lsta_const, gmov_const = sem("lstage_done"), sem("lsta_const"), sem("gmov_const")
        centred, be2_full = sem("centred"), sem("be2_full")
        we2T_full, we2T_done = sem("we2T_full"), sem("we2T_done")
        fold_full, fold_done = sem("fold_full"), sem("fold_done")
        x_in = [sem(f"x_in{n}") for n in range(RING)]
        adj_in = [sem(f"adj_in{n}") for n in range(2)]
        ab_stored = sem("ab_stored")
        s_stored = sem("s_stored")
        w_stored = sem("w_stored")
        g_in = [sem(f"g_in{n}") for n in range(2)]
        l_in = [sem(f"l_in{n}") for n in range(2)]
        rwa_in = [sem(f"rwa_in{n}") for n in range(2)]
        out_stored = [sem(f"out_stored{n}") for n in range(2)]
        xT_full, xT_done = sem("xT_full"), sem("xT_done")
        ab_full, hi_done, lo_done = sem("ab_full"), sem("hi_done"), sem("lo_done")
        abT_full, abT_done, sq_done = sem("abT_full"), sem("abT_done"), sem("sq_done")
        v_full, ve_done, y_done = sem("v_full"), sem("ve_done"), sem("y_done")
        r_done, s_done, w_done = sem("r_done"), sem("s_done"), sem("w_done")
        rw_full, rwT_done = sem("rw_full"), sem("rwT_done")
        hx2_done, xb_done, wsel_done = sem("hx2_done"), sem("xb_done"), sem("wsel_done")
        u_full, z_done, g_done, sum_done = sem("u_full"), sem("z_done"), sem("g_done"), sem("sum_done")
        ms_done, mT_full, mT_done = sem("ms_done"), sem("mT_full"), sem("mT_done")
        h_full, h_read, mv_done, rstd_done = sem("h_full"), sem("h_read"), sem("mv_done"), sem("rstd_done")
        n1_done, n1T_full, g2_done = sem("n1_done"), sem("n1T_full"), sem("g2_done")
        y_full, out_done = sem("y_full"), sem("out_done")
        s_hi = sem("s_hi")
        dve_step, pool_step = sem("dve_step"), sem("pool_step")
        dve_stats, pool_newton, pool_hx, pool_rstd = (
            sem("dve_stats"), sem("pool_newton"), sem("pool_hx"), sem("pool_rstd"))

        x_v = x.rearrange("(k par) i f -> k (par i) f", par=2)
        adj_v = adj.rearrange("(k par) i j -> k (par i) j", par=2)
        out_v = out.rearrange("(k par) i f -> k (par i) f", par=2)

        def at(view, k):
            if not k.looped:
                return view[k.c]
            v = view[bass.ds(k.number(), 1)]
            names = " ".join("abcdef"[: len(view.shape) - 1])
            return v.rearrange(f"z {names} -> (z {names.split()[0]}) {' '.join(names.split()[1:])}")

        def row(v):
            return v.unsqueeze(0).to_broadcast([128, D])

        def col(v):
            return v.rearrange("(p o) -> p o", o=1)

        first_weights = ((w1[:, 0], We1[0:D]), (w1[:, 1], We1[D:2 * D]), (be1_r, row(be1)), (ge_r, row(ge)),
                         (cols[:, 0:1], col(be1)), (wn1[:, 0], Wn1[0:D]), (bge_r, row(bge)))
        later_weights = ((we2[:], We2), (wn1[:, 1], Wn1[D:2 * D]), (cols[:, 3:4], col(be2)), (bn1_r, row(bn1)),
                         (bn2_r, row(bn2)), (wn2[:], Wn2), (cols[:, 1:2], col(gn)), (cols[:, 2:3], col(bgn)))
        ALL_FIRST, ALL_LATER = 16 * len(first_weights), 16 * len(later_weights)

        block = ctx.enter_context(nc.Block())

        @block.sync
        def _(sp):
            def load_x(k):
                if k.looped or k.c >= RING:
                    sp.wait_ge(xb_done, (k - RING).count())
                sp.dma_start(xin[:, k.ring(RING), :], at(x_v, k)).then_inc(x_in[k.ring(RING)], 16)

            def load_adj(k):
                if k.looped or k.c >= 2:
                    sp.wait_ge(w_done, (k - 2).count())
                sp.dma_start(adjin[:, k.ring(2), :], at(adj_v, k)).then_inc(adj_in[k.ring(2)], 16)

            def load_g(k):
                if k.looped or k.c >= 2:
                    sp.wait_ge(z_done, (k - 2).unit_count(UNITS - 1))
                if not k.looped:
                    sp.wait_ge(gmov_const, 1)
                    sp.wait_ge(lsta_const, 2)
                    sp.wait_ge(ab_stored, k.count(64))
                gv = gmov[k.ring(2)][:].bitcast(F32)
                for half in range(2):
                    sp.dma_start(gv[K_B:K_A, :, 2 * half * D:2 * (half + 1) * D],
                                 at(store_b, k)).then_inc(g_in[k.ring(2)], 16)
                src = at(store_a, k).rearrange("q par tl f -> q (par tl f)").unsqueeze(1)
                sp.dma_start(gv[K_A:K_S].rearrange("q (h par) x -> q h (par x)", h=2),
                             src.to_broadcast([32, 2, 2 * 4 * D])).then_inc(g_in[k.ring(2)], 16)

            def load_s(k):
                sp.wait_ge(s_stored, k.count(16))
                lv = lsta[k.ring(2)][:].bitcast(F32)
                sv = at(store_s, k)
                for par in range(2):
                    sp.dma_start(lv[K_S:K_E, par],
                                 sv[:, par].rearrange("c (tl r) j -> c tl (r j)", tl=4)).then_inc(l_in[k.ring(2)], 16)

            def store_rw(k):
                sp.wait_ge(rwT_done, k.count())
                sp.dma_start(at(store_w, k).rearrange("p q e -> q p e"), rwT[:]).then_inc(w_stored, 16)

            def load_rw(k):
                if not k.looped and k.c >= 2:
                    sp.wait_ge(wsel_done, (k - 2).count())
                sp.wait_ge(w_stored, k.count(16))
                sp.dma_start(rwa[k.ring(2)][:].rearrange("q a e -> q (a e)"),
                             at(store_w, k).rearrange("p (jl a) e -> (p jl) (a e)", a=4)).then_inc(rwa_in[k.ring(2)], 16)

            def store_ab(k):
                sp.wait_ge(lo_done, k.count())
                for hl in range(2):
                    dst = at(store_a, k)[16 * hl:16 * hl + 16].rearrange("r par tl f -> (par tl) r f")
                    sp.dma_start(dst, a_hl[:, hl, :].bitcast(F32)).then_inc(ab_stored, 16)
                    dst = at(store_b, k)[32 * hl:32 * hl + 32].rearrange("jl hp f -> hp jl f")
                    sp.dma_start(dst, b_hl[:, hl].bitcast(F32).rearrange("q r f -> q (r f)")).then_inc(ab_stored, 16)

            def store_std(k):
                sp.wait_ge(s_done, k.count())
                sp.dma_start(at(store_s, k).rearrange("c par i j -> (par i) c j"),
                             s_hl[:].bitcast(F32)).then_inc(s_stored, 16)

            def store_out(k):
                sp.wait_ge(out_done, k.count())
                sp.dma_start(at(out_v, k), outs[:, k.ring(2), :]).then_inc(out_stored[k.ring(2)], 16)

            for dst, src in first_weights:
                sp.dma_start(dst, src).then_inc(first_in, 16)
            load_x(Pair(0))
            load_adj(Pair(0))
            load_x(Pair(1))
            for dst, src in later_weights:
                sp.dma_start(dst, src).then_inc(weights_in, 16)
            load_x(Pair(2))
            load_adj(Pair(1))
            load_x(Pair(3))
            store_ab(Pair(0))
            load_g(Pair(0))
            store_ab(Pair(1))
            store_rw(Pair(0))
            store_std(Pair(0))
            load_rw(Pair(0))
            load_s(Pair(0))
            load_adj(Pair(2))
            store_ab(Pair(2))
            store_std(Pair(1))

            def iteration(k):
                if (k + 1).exists():
                    load_g(k + 1)
                    store_rw(k + 1)
                    load_s(k + 1)
                if (k + 4).exists():
                    load_x(k + 4)
                if (k + 3).exists():
                    load_adj(k + 3)
                if (k + 1).exists():
                    load_rw(k + 1)
                if (k + 3).exists():
                    store_ab(k + 3)
                if (k + 2).exists():
                    store_std(k + 2)
                if (k - 2).exists():
                    store_out(k - 2)

            schedule(sp, iteration)
            for n in range(2):
                sp.wait_ge(out_stored[n], PAIRS // 2 * 16)

        @block.gpsimd
        def _(pool):
            steps = [0]

            def link(ins):
                steps[0] += 1
                ins.then_inc(pool_step, 1)
                pool.wait_ge(pool_step, steps[0])

            def select(view, base, pattern):
                link(nc.gpsimd.affine_select(out=view, in_=view, compare_op=ALU.not_equal, fill=1.0,
                                             base=base, pattern=pattern, channel_multiplier=1))

            link(nc.gpsimd.memset(ident[:], 0.0))
            nc.gpsimd.affine_select(out=ident[:], in_=ident[:], compare_op=ALU.not_equal, fill=1.0, base=0,
                                    pattern=[[-1, 128]], channel_multiplier=1).then_inc(ident_done, 1)
            for view, value in ((ones_a, 1.0 / D), (ones_b, 64.0 * 64.0 / D), (ones, 1.0), (three_halves, 1.5),
                                (halves, -0.5), (eps, EPS), (minus_half, -0.5), (offdiag, 1.0), (rowmask, 0.0)):
                ins = nc.gpsimd.memset(view[:], value)
            link(ins)
            for par in range(2):
                v = offdiag[64 * par:64 * par + 64, :]
                link(nc.gpsimd.affine_select(out=v, in_=v, compare_op=ALU.not_equal, fill=0.0, base=0,
                                             pattern=[[-1, N]], channel_multiplier=1))
            for m, offs in ((0, (0, 8)), (1, (4, 12))):
                for off in offs:
                    select(rowmask[96:128, m, :], -off, [[-1, 4]])
            for m, off in ((2, 16), (3, 17)):
                select(rowmask[96:128, m, :], -off, [[0, 4]])
            nc.gpsimd.memset(pmask[:], 0.0).then_inc(pool_const, 1)
            pool.wait_ge(pool_const, 1)
            for p in range(4):
                link(nc.gpsimd.memset(pmask[32 * p:32 * p + 32, p:p + 1], 1.0))
            nc.gpsimd.memset(wsel[0][:], 0.0)
            link(nc.gpsimd.memset(wsel[1][:], 0.0))

            def squares(k):
                pool.wait_ge(abT_done, k.count())
                if (k - 1).exists():
                    pool.wait_ge(v_full, (k - 1).count())
                nc.gpsimd.tensor_tensor(sq[:], abT[:], abT[:], ALU.mult).then_inc(sq_done, 1)

            def newton(k):
                pool.wait_ge(y_done, k.count())
                done = 0

                def step(ins):
                    nonlocal done
                    done += 1
                    ins.then_inc(pool_newton, 1)
                    pool.wait_ge(pool_newton, (k - 1).count(13) + done)

                nc.gpsimd.tensor_tensor(vh[:], ve[:], halves[:], ALU.mult)
                for it in range(3):
                    step(nc.gpsimd.tensor_tensor(nt[:, 0], y[:], y[:], ALU.mult))
                    step(nc.gpsimd.tensor_tensor(nt[:, 1], nt[:, 0], vh[:], ALU.mult))
                    step(nc.gpsimd.tensor_tensor(nt[:, 0], nt[:, 1], three_halves[:], ALU.add))
                    step(nc.gpsimd.tensor_tensor(y[:], y[:], nt[:, 0], ALU.mult))
                if (k - 1).exists():
                    pool.wait_ge(rw_full, (k - 1).count())
                    pool.wait_ge(s_stored, (k - 1).count(16))
                nc.gpsimd.tensor_tensor(rw[:, :, 0, :], y[:].rearrange("q (jl h) -> q jl h", h=2),
                                        ones[:].rearrange("q (jl h) -> q jl h", h=2), ALU.mult).then_inc(r_done, 1)
                nc.gpsimd.tensor_tensor(std[:], ve[:], y[:], ALU.mult).then_inc(pool_newton, 1)
                twice = std[:].unsqueeze(1).to_broadcast([128, 2, N])
                nc.gpsimd.tensor_tensor(s_hl[:, 0:2], ve[:].unsqueeze(1).to_broadcast([128, 2, N]),
                                        y[:].unsqueeze(1).to_broadcast([128, 2, N]), ALU.mult).then_inc(s_hi, 1)
                pool.wait_ge(pool_newton, k.count(13))
                pool.wait_ge(s_hi, k.count())
                nc.gpsimd.tensor_tensor(s_hl[:, 2:4], twice, s_hl[:, 0:2].bitcast(F32),
                                        ALU.subtract).then_inc(s_done, 1)

            def node_bias(k):
                pool.wait_ge(hi_done, k.count())
                pool.wait_ge(w_done, k.count())
                nc.gpsimd.tensor_tensor(vw[:, k.ring(2), :], v_r[:], sumw[:, k.ring(2):k.ring(2) + 1].to_broadcast([128, D]),
                                        ALU.mult).then_inc(pool_hx, 1)
                pool.wait_ge(pool_hx, (k - 1).count(2) + 1)
                nc.gpsimd.tensor_tensor(vw[:, k.ring(2), :], vw[:, k.ring(2), :], bn1_r, ALU.add).then_inc(pool_hx, 1)
                pool.wait_ge(pool_hx, k.count(2))
                if (k - RING).exists() or k.looped:
                    pool.wait_ge(h_read, (k - RING).count())
                nc.gpsimd.tensor_tensor(hx2[:, k.ring(RING), :], hx[:, k.ring(RING), :], vw[:, k.ring(2), :],
                                        ALU.add).then_inc(hx2_done, 1)

            def select_weights(k):
                pool.wait_ge(rwa_in[k.ring(2)], k.count2(16))
                if (k - 2).exists() or k.looped:
                    pool.wait_ge(sum_done, (k - 2).unit_count(UNITS - 1))
                w = rwa[k.ring(2)][:, 2:4, :].rearrange("q h e -> q (h e)")
                nc.gpsimd.tensor_tensor(wsel[k.ring(2)][:, :, 0:4],
                                        w.unsqueeze(2).to_broadcast([128, UNITS * TILES, 4]),
                                        pmask[:].unsqueeze(1).to_broadcast([128, UNITS * TILES, 4]),
                                        ALU.mult).then_inc(wsel_done, 1)

            def residual(k):
                pool.wait_ge(x_in[k.ring(RING)], k.count4(16))
                pool.wait_ge(xT_full, k.count())
                if (k - RING).exists() or k.looped:
                    pool.wait_ge(out_done, (k - RING).count())
                nc.gpsimd.tensor_tensor(xb[:, k.ring(RING), :], xin[:, k.ring(RING), :], bn2_r,
                                        ALU.add).then_inc(xb_done, 1)

            def node_rstd(k):
                pool.wait_ge(mv_done, k.count())
                nc.gpsimd.tensor_tensor(vpe[:], mv[:, 1:2], eps[:], ALU.add).then_inc(pool_rstd, 1)
                pool.wait_ge(pool_rstd, k.count())
                if (k - 1).exists():
                    pool.wait_ge(n1_done, (k - 1).count())
                nc.gpsimd.tensor_tensor(rstd[:], vpe[:], minus_half[:], ALU.pow).then_inc(rstd_done, 1)

            squares(Pair(0))
            newton(Pair(0))
            squares(Pair(1))
            newton(Pair(1))
            squares(Pair(2))
            select_weights(Pair(0))
            pool.wait_ge(weights_in, ALL_LATER)
            pool.wait_ge(fold_done, 1)
            for c in range(2):
                node_bias(Pair(c))
                residual(Pair(c))

            def iteration(k):
                if (k - 2).exists():
                    node_rstd(k - 2)
                if (k + 2).exists():
                    newton(k + 2)
                if (k + 2).exists():
                    residual(k + 2)
                if (k + 3).exists():
                    squares(k + 3)
                if (k + 1).exists():
                    select_weights(k + 1)
                if (k + 2).exists():
                    node_bias(k + 2)

            schedule(pool, iteration)

        @block.scalar
        def _(act):
            def copy_xT(k):
                act.wait_ge(xT_full, k.count())
                if (k - 1).exists():
                    act.wait_ge(ab_full, (k - 1).count())
                    act.wait_ge(abT_full, (k - 1).count())
                nc.scalar.copy(xT[:], p1[:, 0:128]).then_inc(xT_done, 1)

            def high_parts(k):
                act.wait_ge(ab_full, k.count())
                if (k - 1).exists():
                    act.wait_ge(ab_stored, (k - 1).count(64))
                if (k - RING).exists() or k.looped:
                    act.wait_ge(hx2_done, (k - RING).count())
                nc.scalar.copy(a_hl[:, 0], p0[:, 0:D])
                nc.scalar.copy(hx[:, k.ring(RING), :], p0[:, D:2 * D])
                nc.scalar.copy(b_hl[:, 0], p0[:, 2 * D:3 * D].unsqueeze(1).to_broadcast([128, 2, D])).then_inc(hi_done, 1)

            def copy_abT(k):
                act.wait_ge(abT_full, k.count())
                if (k - 1).exists():
                    act.wait_ge(v_full, (k - 1).count())
                    act.wait_ge(sq_done, (k - 1).count())
                nc.scalar.activation(abT[:, 0], p1[:, 0:128], ACT.Identity, bias=be1c_col[:])
                nc.scalar.copy(abT[:, 1], p1[:, 128:256]).then_inc(abT_done, 1)

            def copy_rwT(k):
                act.wait_ge(rw_full, k.count())
                if (k - 1).exists():
                    act.wait_ge(w_stored, (k - 1).count(16))
                src = p1[:, 0:128].rearrange("q (pt tq p) -> q p tq pt", pt=8, tq=4)
                nc.scalar.copy(rwT[:].rearrange("q p (tq pt) -> q p tq pt", tq=4), src).then_inc(rwT_done, 1)

            def copy_messages(k):
                act.wait_ge(sum_done, k.unit_count(UNITS - 1))
                if (k - 1).exists():
                    act.wait_ge(mT_full, (k - 1).count())
                nc.scalar.copy(ms[:], msg[k.ring(2)][:, 0:D]).then_inc(ms_done, 1)

            def copy_mT(k):
                act.wait_ge(mT_full, k.count())
                if (k - 1).exists():
                    act.wait_ge(h_full, (k - 1).count())
                nc.scalar.copy(mT[:], p1[:, 0:128]).then_inc(mT_done, 1)

            def node_gelu(k):
                act.wait_ge(n1T_full, k.count())
                if (k - 1).exists():
                    act.wait_ge(y_full, (k - 1).count())
                nc.scalar.activation(g2T[:], p1[:, 0:128], ACT.Gelu, bias=cols[:, 2:3],
                                     scale=cols[:, 1:2]).then_inc(g2_done, 1)

            def edge_gelu(k, u):
                act.wait_ge(z_done, k.unit_count(u))
                if k.looped or k.c * UNITS + u >= GELU_RING:
                    act.wait_ge(sum_done, k.unit_count(u - GELU_RING))
                nc.scalar.activation(g[:, u % GELU_RING], z[:, u % GELU_RING], ACT.Gelu).then_inc(g_done, 1)

            act.wait_ge(ident_done, 1)
            nc.scalar.activation(g[:, 0, 0, :], ident[:], ACT.Gelu)
            act.wait_ge(lstage_done, 1)
            nc.scalar.copy(lsta[1][:], lstage[:].unsqueeze(1).to_broadcast([128, 2, 16 * N])).then_inc(lsta_const, 1)
            copy_xT(Pair(0))
            act.wait_ge(centred, 1)
            copy_abT(Pair(0))
            high_parts(Pair(0))
            copy_xT(Pair(1))
            copy_abT(Pair(1))
            high_parts(Pair(1))
            copy_rwT(Pair(0))
            act.wait_ge(we2T_full, 1)
            nc.scalar.copy(we2T[:], p1[:, 0:128]).then_inc(we2T_done, 1)
            copy_xT(Pair(2))
            copy_abT(Pair(2))
            high_parts(Pair(2))
            act.wait_ge(weights_in, ALL_LATER)

            def iteration(k):
                for u in range(UNITS):
                    if k.exists():
                        edge_gelu(k, u)
                    if u == 1 and (k + 1).exists():
                        copy_rwT(k + 1)
                    if u == 1 and (k + 3).exists():
                        copy_xT(k + 3)
                    if u == 2 and (k - 1).exists():
                        copy_messages(k - 1)
                    if u == 3 and (k + 3).exists():
                        high_parts(k + 3)
                    if u == 3 and (k - 2).exists():
                        node_gelu(k - 2)
                    if u == 3 and (k - 1).exists():
                        copy_mT(k - 1)
                    if u == 6 and (k + 3).exists():
                        copy_abT(k + 3)

            schedule(act, iteration)

        @block.vector
        def _(dve):
            steps = [0]

            def link(ins):
                steps[0] += 1
                ins.then_inc(dve_step, 1)
                dve.wait_ge(dve_step, steps[0])

            def low_parts(k):
                dve.wait_ge(hi_done, k.count())
                nc.vector.tensor_tensor(a_hl[:, 1], p0[:, 0:D], a_hl[:, 0].bitcast(F32), ALU.subtract)
                nc.vector.tensor_tensor(b_hl[:, 1], p0[:, 2 * D:3 * D].unsqueeze(1).to_broadcast([128, 2, D]),
                                        b_hl[:, 0].bitcast(F32), ALU.subtract).then_inc(lo_done, 1)

            def weights(k):
                dve.wait_ge(adj_in[k.ring(2)], k.count2(16))
                if (k - 1).exists():
                    dve.wait_ge(rw_full, (k - 1).count())
                if (k - 2).exists() or k.looped:
                    dve.wait_ge(hx2_done, (k - 2).count())
                nc.vector.scalar_tensor_tensor(
                    out=rw[:, :, 1, :], in0=adjin[:, k.ring(2), :].rearrange("q (jl h) -> q jl h", h=2), scalar=1.0,
                    in1=offdiag[:].rearrange("q (jl h) -> q jl h", h=2), op0=ALU.mult, op1=ALU.mult,
                    accum_out=sumw[:, k.ring(2):k.ring(2) + 1]).then_inc(w_done, 1)

            def variance(k):
                dve.wait_ge(v_full, k.count())
                if (k - 1).exists():
                    dve.wait_ge(s_done, (k - 1).count())
                nc.vector.tensor_scalar(ve[:], p0[:, 0:N], 0.0, EPS, ALU.max, ALU.add).then_inc(ve_done, 1)

            def first_guess(k):
                dve.wait_ge(ve_done, k.count())
                nc.vector.tensor_scalar(y[:].bitcast(I32), ve[:].bitcast(I32), -0.5, float(RSQRT_MAGIC), ALU.mult,
                                        ALU.add).then_inc(y_done, 1)

            def node_sum(k):
                dve.wait_ge(h_full, k.count())
                dve.wait_ge(hx2_done, k.count())
                nc.vector.tensor_tensor(hpre[:], p0[:, 0:D], hx2[:, k.ring(RING), :], ALU.add).then_inc(h_read, 1)

            def node_stats(k):
                dve.wait_ge(h_read, k.count())
                nc.vector.bn_stats(stats[:], hpre[:]).then_inc(dve_stats, 1)

            def weights_and_mean(k_w, k):
                if k.exists():
                    dve.wait_ge(dve_stats, k.count())
                    if (k - 1).exists():
                        dve.wait_ge(rstd_done, (k - 1).count())
                if k_w.exists():
                    weights(k_w)
                if k.exists():
                    nc.vector.bn_aggr(mv[:], stats[:]).then_inc(mv_done, 1)

            def normalise(k):
                dve.wait_ge(rstd_done, k.count())
                if (k - 1).exists():
                    dve.wait_ge(n1T_full, (k - 1).count())
                nc.vector.tensor_scalar(n1[:], hpre[:], mv[:, 0:1], rstd[:], ALU.subtract,
                                        ALU.mult).then_inc(n1_done, 1)

            def finish(k):
                dve.wait_ge(y_full, k.count())
                dve.wait_ge(xb_done, k.count())
                if (k - 2).exists() or k.looped:
                    dve.wait_ge(out_stored[k.ring(2)], (k - 2).count2(16))
                nc.vector.tensor_tensor(outs[:, k.ring(2), :], p0[:, 0:D], xb[:, k.ring(RING), :],
                                        ALU.add).then_inc(out_done, 1)

            def scale(k, u):
                dve.wait_ge(u_full, k.unit_count(u))
                if u == 0:
                    dve.wait_ge(rwa_in[k.ring(2)], k.count2(16))
                if k.looped or k.c * UNITS + u >= GELU_RING:
                    dve.wait_ge(g_done, k.unit_count(u - GELU_RING))
                h, tq = divmod(u, 4)
                r = rwa[k.ring(2)][:, h, TILES * tq:TILES * (tq + 1)]
                nc.vector.tensor_tensor(z[:, u % GELU_RING], up[u % 2][:],
                                        r.unsqueeze(2).to_broadcast([128, TILES, D]), ALU.mult).then_inc(z_done, 1)

            dve.wait_ge(ident_done, 1)
            nc.vector.tensor_tensor(sel[0:64, 0:32], ident[0:64, 0:32], ident[0:64, 32:64], ALU.add)
            link(nc.vector.tensor_tensor(sel[64:96, 0:16], ident[64:96, 64:80], ident[64:96, 80:96], ALU.add))
            nc.vector.tensor_copy(lstage[0:64, :].rearrange("q (r jl h) -> q r jl h", jl=32, h=2),
                                  sel[0:64, 0:32].unsqueeze(1).unsqueeze(3).to_broadcast([64, 16, 32, 2]))
            nc.vector.tensor_copy(lstage[64:96, :].rearrange("q (r j) -> q r j", j=N),
                                  sel[64:96, 0:16].unsqueeze(2).to_broadcast([32, 16, N]))
            nc.vector.memset(lstage[96:128, :], 1.0).then_inc(lstage_done, 1)
            dve.wait_ge(lstage_done, 1)
            nc.vector.tensor_copy(lsta[0][:], lstage[:].unsqueeze(1).to_broadcast([128, 2, 16 * N])).then_inc(lsta_const, 1)
            dve.wait_ge(first_in, ALL_FIRST)
            nc.vector.reduce_sum(mean[:, 0:2], w1[:], axis=AXX)
            link(nc.vector.reduce_sum(mean[:, 2:3], be1_r, axis=AXX))
            link(nc.vector.tensor_scalar(mean[:], mean[:], 1.0 / D, None, ALU.mult))
            nc.vector.tensor_scalar(w1[:, 1], w1[:, 1], mean[:, 1:2], None, ALU.subtract)
            nc.vector.tensor_scalar(w1c[:, 0], w1[:, 0], mean[:, 0:1], None, ALU.subtract)
            nc.vector.tensor_scalar(be1c_r[:], be1_r, mean[:, 2:3], None, ALU.subtract)
            link(nc.vector.tensor_scalar(be1c_col[:], cols[:, 0:1], mean[:, 2:3], None, ALU.subtract))
            nc.vector.tensor_scalar(w1c[:, 1], w1[:, 1], 1.0 / 64, None, ALU.mult)
            nc.vector.tensor_tensor(w_ah[:, 0], w1c[:, 0], ge_r, ALU.mult)
            nc.vector.tensor_copy(w_ah[:, 1], wn1[:, 0])
            nc.vector.tensor_tensor(w_b[:], w1[:, 1], ge_r, ALU.mult).then_inc(centred, 1)
            link(nc.vector.tensor_tensor(be1c_r[:], be1c_r[:], ge_r, ALU.mult))
            sources = ((0, bge_r), (2, be1c_r[:]))
            for m, src in sources:
                last = nc.vector.tensor_copy(bias_hl[:, m], src)
            link(last)
            for m, src in sources:
                nc.vector.tensor_tensor(bias_hl[:, m + 1], src, bias_hl[:, m].bitcast(F32), ALU.subtract)
            link(nc.vector.memset(sumw[:], 0.0))
            dve.wait_ge(pool_const, 1)
            weights(Pair(0))
            q = slice(K_S, 128)
            bias = [bias_hl[q, m].bitcast(F32) for m in range(4)]
            link(nc.vector.tensor_scalar(grow[q, 0], bias[2], rowmask[q, 2, 0:1], None, ALU.mult))
            link(nc.vector.scalar_tensor_tensor(out=grow[q, 1], in0=bias[3], scalar=rowmask[q, 3, 0:1],
                                                in1=grow[q, 0], op0=ALU.mult, op1=ALU.add))
            for m in range(2):
                for tl in range(4):
                    last = nc.vector.scalar_tensor_tensor(
                        out=gconst[q, tl], in0=bias[m], scalar=rowmask[q, m, tl:tl + 1],
                        in1=gconst[q, tl] if m else grow[q, 1], op0=ALU.mult, op1=ALU.add)
                link(last)
                if m == 0:
                    low_parts(Pair(0))
            variance(Pair(0))
            first_guess(Pair(0))
            for n in range(2):
                last = nc.vector.tensor_copy(
                    gmov[n][q], gconst[q].rearrange("q t f -> q (t f)").unsqueeze(1).to_broadcast([32, 4, 4 * D]))
            last.then_inc(gmov_const, 1)
            dve.wait_ge(weights_in, ALL_LATER)
            nc.vector.tensor_copy(be2_bc[:], cols[:, 3:4].to_broadcast([128, 128])).then_inc(be2_full, 1)
            low_parts(Pair(1))
            weights(Pair(1))
            variance(Pair(1))
            first_guess(Pair(1))
            dve.wait_ge(fold_full, 1)
            nc.vector.tensor_copy(wc[:], p0[:, 0:D])
            nc.vector.tensor_copy(v_r[:], p0[:, D:2 * D]).then_inc(fold_done, 1)
            low_parts(Pair(2))

            def iteration(k):
                for u in range(UNITS):
                    if k.exists():
                        scale(k, u)
                    if u == 0 and (k - 2).exists():
                        node_sum(k - 2)
                    if u == 1 and (k - 2).exists():
                        node_stats(k - 2)
                    if u == 2 and (k + 2).exists():
                        variance(k + 2)
                    if u == 2:
                        weights_and_mean(k + 2, k - 2)
                    if u == 3 and (k + 2).exists():
                        first_guess(k + 2)
                    if u == 4 and (k - 2).exists():
                        normalise(k - 2)
                    if u == 5 and (k + 3).exists():
                        low_parts(k + 3)
                    if u == 7 and (k - 2).exists():
                        finish(k - 2)

            schedule(dve, iteration)

        @block.tensor
        def _(pe):
            def transpose_x(k, free=None):
                pe.wait_ge(x_in[k.ring(RING)], k.count4(16))
                if free:
                    pe.wait_ge(*free)
                nc.tensor.transpose(p1[:, 0:128], xin[:, k.ring(RING), :], ident[:]).then_inc(xT_full, 1)

            def node_products(k, free=None):
                pe.wait_ge(xT_done, k.count())
                if free:
                    pe.wait_ge(*free)
                nc.tensor.matmul(p0[:, 0:2 * D], xT[:], w_ah[:].rearrange("q a f -> q (a f)"), start=True, stop=True)
                by_h = xT[:].rearrange("q (m h) -> q h m", h=2)
                for h in range(2):
                    last = nc.tensor.matmul(p0[64 * h:64 * h + 64, 2 * D:3 * D], by_h[:, h], w_b[:],
                                            start=True, stop=True)
                last.then_inc(ab_full, 1)

            def feature_products(k, free=None):
                pe.wait_ge(xT_done, k.count())
                if free:
                    pe.wait_ge(*free)
                nc.tensor.matmul(p1[:, 0:128], w1c[:, 0], xT[:], start=True, stop=True)
                nc.tensor.matmul(p1[:, 128:256], w1c[:, 1], xT[:], start=True, stop=True).then_inc(abT_full, 1)

            def variances(k, free):
                pe.wait_ge(sq_done, k.count())
                pe.wait_ge(*free)
                terms = ((lambda s: abT[:, 0, s], lambda s: abT[:, 1, s]),
                         (lambda s: sq[:, 0, s], lambda s: ones_a[:]),
                         (lambda s: ones_b[:], lambda s: sq[:, 1, s]))
                for t, (left, right) in enumerate(terms):
                    for par in range(2):
                        s = slice(64 * par, 64 * par + 64)
                        last = nc.tensor.matmul(p0[s, 0:N], left(s), right(s), start=(t == 0), stop=(t == 2))
                last.then_inc(v_full, 1)

            def transpose_rw(k, free):
                pe.wait_ge(r_done, k.count())
                pe.wait_ge(w_done, k.count())
                if free:
                    pe.wait_ge(*free)
                nc.tensor.transpose(p1[:, 0:128], rw[:].rearrange("q jl a h -> q (jl a h)"), ident[:]).then_inc(rw_full, 1)

            def u_product(k, u):
                if u == 0:
                    pe.wait_ge(g_in[k.ring(2)], k.count2(48))
                    pe.wait_ge(l_in[k.ring(2)], k.count2(32))
                if k.looped or k.c * UNITS + u >= 2:
                    pe.wait_ge(z_done, k.unit_count(u - 2))
                h, tq = divmod(u, 4)
                for par in range(2):
                    selector = lsta[k.ring(2)][0:K_ROWS, par, 256 * tq:256 * tq + 256].rearrange("q (e h) -> q h e", h=2)
                    last = nc.tensor.matmul(up[u % 2][:, 4 * par:4 * par + 4, :].rearrange("q t f -> q (t f)"),
                                            selector[:, h],
                                            gmov[k.ring(2)][0:K_ROWS, 2 * h + par, :], start=True, stop=True)
                last.then_inc(u_full, 1)

            def weighted_sum(k, u):
                pe.wait_ge(g_done, k.unit_count(u))
                if u == 0:
                    pe.wait_ge(wsel_done, k.count())
                    if (k - 2).exists() or k.looped:
                        pe.wait_ge(ms_done, (k - 2).count())
                tq = u % 4
                ws = wsel[k.ring(2)][:].rearrange("q t s -> q (t s)")
                for tl0 in range(2):
                    for c in range(4):
                        tile = 4 * (c // 2) + 2 * (c % 2) + tl0
                        at0 = SLOT * (TILES * u + tile) - 16 * tl0 - 4 * tq
                        last = nc.tensor.matmul(msg[k.ring(2)][32 * c:32 * c + 32, 0:D], ws[:, at0:at0 + 32],
                                                g[:, u % GELU_RING, tile, :], start=(u == 0 and tl0 == 0),
                                                stop=(u == UNITS - 1 and tl0 == 1))
                last.then_inc(sum_done, 1)

            def transpose_messages(k, free):
                pe.wait_ge(ms_done, k.count())
                pe.wait_ge(*free)
                nc.tensor.transpose(p1[:, 0:128], ms[:], ident[:]).then_inc(mT_full, 1)

            def node_hidden(k, free):
                pe.wait_ge(mT_done, k.count())
                pe.wait_ge(*free)
                nc.tensor.matmul(p0[:, 0:D], mT[:], wc[:], start=True, stop=True).then_inc(h_full, 1)

            def transpose_n1(k, free):
                pe.wait_ge(n1_done, k.count())
                pe.wait_ge(*free)
                nc.tensor.transpose(p1[:, 0:128], n1[:], ident[:]).then_inc(n1T_full, 1)

            def node_output(k, free):
                pe.wait_ge(g2_done, k.count())
                pe.wait_ge(*free)
                nc.tensor.matmul(p0[:, 0:D], g2T[:], wn2[:], start=True, stop=True).then_inc(y_full, 1)

            pe.wait_ge(ident_done, 1)
            transpose_x(Pair(0))
            pe.wait_ge(centred, 1)
            feature_products(Pair(0), (xT_done, 1))
            pe.wait_ge(pool_const, 1)
            node_products(Pair(0))
            transpose_x(Pair(1), (abT_done, 1))
            variances(Pair(0), (lo_done, 1))
            feature_products(Pair(1), (xT_done, 2))
            node_products(Pair(1), (ve_done, 1))
            transpose_rw(Pair(0), (abT_done, 2))
            variances(Pair(1), (lo_done, 2))
            pe.wait_ge(weights_in, ALL_LATER)
            pe.wait_ge(rwT_done, 1)
            nc.tensor.transpose(p1[:, 0:128], we2[:], ident[:]).then_inc(we2T_full, 1)
            transpose_x(Pair(2), (we2T_done, 1))
            pe.wait_ge(ve_done, 2)
            pe.wait_ge(be2_full, 1)
            nc.tensor.matmul(p0[:, 0:D], we2T[:], wn1[:, 1], start=True, stop=True)
            nc.tensor.matmul(p0[:, D:2 * D], be2_bc[:], wn1[:, 1], start=True, stop=True).then_inc(fold_full, 1)
            feature_products(Pair(2), (xT_done, 3))
            node_products(Pair(2), (fold_done, 1))

            def iteration(k):
                nxt, two, three, prev, old = (k + 1).exists(), (k + 2).exists(), (k + 3).exists(), k - 1, k - 2
                for u in range(UNITS):
                    if k.exists():
                        u_product(k, u)
                    w = u - W_LAG
                    if w >= 0 and k.exists():
                        weighted_sum(k, w)
                    if w < 0 and prev.exists():
                        weighted_sum(prev, w + UNITS)
                    if u == 0 and old.exists():
                        node_hidden(old, (out_done, (k - 3).count()) if (k - 3).exists()
                                         else (lo_done, (k + 2).count()))
                    if u == 1 and nxt:
                        transpose_rw(k + 1, (abT_done, (k + 2).count()) if two
                                            else (mT_done, old.count()))
                    if u == 2 and two:
                        variances(k + 2, (h_read, old.count()) if old.exists()
                                         else (lo_done, (k + 2).count()))
                    if u == 3 and three:
                        transpose_x(k + 3, (rwT_done, (k + 1).count()))
                    if u == 4 and three:
                        node_products(k + 3, (ve_done, (k + 2).count()))
                    if u == 5 and old.exists():
                        transpose_n1(old, (xT_done, (k + 3).count()) if three
                                          else (rwT_done, (k + 1).count()) if nxt
                                          else (mT_done, old.count()))
                    if u == 6 and prev.exists():
                        transpose_messages(prev, (g2_done, old.count()) if old.exists()
                                                 else (xT_done, (k + 3).count()))
                    if u == 7 and three:
                        feature_products(k + 3, (mT_done, prev.count()) if prev.exists()
                                                else (xT_done, (k + 3).count()))
                    if u == 7 and old.exists():
                        node_output(old, (lo_done, (k + 3).count()) if three
                                         else (ve_done, (k + 2).count()) if two
                                         else (h_read, old.count()))

            schedule(pe, iteration)


_WEIGHTS = ['We1', 'be1', 'ge', 'bge', 'We2', 'be2', 'Wn1', 'bn1', 'gn', 'bgn', 'Wn2', 'bn2']


def kernel(x, adj, **weights):
    import concourse.bacc as _bacc
    from concourse.bass_utils import run_bass_kernel_spmd as _run

    given = {"x": x, "adj": adj} | {name: weights[f"L0_gnn_{name}"] for name in _WEIGHTS}
    nc = _bacc.Bacc("TRN2", target_bir_lowering=False, num_devices=1)
    arrays, args = {}, []
    for name, a in given.items():
        a = np.ascontiguousarray(a)
        arrays[f"in_{name}"] = a
        args.append(nc.dram_tensor(f"in_{name}", a.shape, mybir.dt.from_np(a.dtype), kind="ExternalInput").ap())
    args.append(nc.dram_tensor("out_x", (B, N, D), F32, kind="ExternalOutput").ap())
    build(nc, *args)
    r = _run(nc, [arrays], core_ids=[0])
    return r.results[0]["out_x"]
```

```python
from contextlib import ExitStack

import numpy as np

import concourse.bass as bass
from concourse import mybir

F32 = mybir.dt.float32
F32R = mybir.dt.float32r
I32 = mybir.dt.int32
ALU = mybir.AluOpType
ACT = mybir.ActivationFunctionType
AXX = mybir.AxisListType.X

B, N, D = 128, 64, 128
PAIRS = B // 2
EPS = 1e-5
UNITS = 8
TILES = 8
K_B, K_A, K_S, K_E = 0, 64, 96, 112
K_ROWS = 114
SLOT = 48
W_LAG = 4
GELU_RING = 8
RING = 4
BODY = 8
FIRST, LAST = 4, 60
NEWTON_C = (0.5 ** (1 / 3), 1.0, 2.0)
R_SCALE = 16.0
RSQRT_MAGIC = 0x5F3759DF - 2 ** 23 / 3


class Pair:

    def __init__(self, c, turn=0, looped=False):
        self.c, self.turn, self.looped = c, turn, looped

    def __add__(self, d):
        return Pair(self.c + d, self.turn, self.looped)

    def __sub__(self, d):
        return self + (-d)

    def exists(self):
        return self.looped or 0 <= self.c < PAIRS

    def number(self):
        return self.turn * BODY + self.c

    def ring(self, n):
        return self.c % n

    def count(self, each=1):
        return self.turn * (BODY * each) + (self.c + 1) * each

    def count2(self, each):
        return self.turn * (BODY // 2 * each) + (self.c // 2 + 1) * each

    def count4(self, each):
        return self.turn * (BODY // 4 * each) + (self.c // 4 + 1) * each

    def unit_count(self, u):
        return self.turn * (BODY * UNITS) + self.c * UNITS + u + 1


def schedule(engine, iteration):
    for c in range(FIRST):
        iteration(Pair(c))
    with engine.Fori(0, (LAST - FIRST) // BODY) as turn:
        for c in range(BODY):
            iteration(Pair(FIRST + c, turn, True))
    for c in range(LAST, PAIRS + 2):
        iteration(Pair(c))


def build(nc, x, adj, We1, be1, ge, bge, We2, be2, Wn1, bn1, gn, bgn, Wn2, bn2, out):
    ctx = ExitStack()
    with ctx:
        def sb(name, shape, dt=F32):
            return ctx.enter_context(nc.sbuf_tensor(name, shape, dt))

        def pb(name, shape):
            return ctx.enter_context(nc.psum_tensor(name, shape, F32))

        def sem(name):
            return ctx.enter_context(nc.semaphore(name))

        def dram(name, shape):
            return nc.dram_tensor(name, shape, F32, kind="Internal").ap()

        store_a = dram("store_a", (PAIRS, 32, 2, 4, D))
        store_b = dram("store_b", (PAIRS, 2, 128, 4 * D))
        store_s = dram("store_s", (PAIRS, 4, 2, N, N))
        store_w = dram("store_w", (PAIRS, 4, 128, 32))

        ident = sb("ident", [128, 128])
        w1 = sb("w1", [128, 2, D])
        wn1 = sb("wn1", [128, 2, D])
        we2 = sb("we2", [128, D])
        we2T = sb("we2T", [128, D])
        wn2 = sb("wn2", [128, D])
        rows = sb("rows", [128, 5, D])
        be1_r, ge_r, bge_r, bn1_r, bn2_r = (rows[:, n, :] for n in range(5))
        cols = sb("cols", [128, 4])
        mean = sb("mean", [128, 6])
        w1c = sb("w1c", [128, 2, D])
        w_hab = sb("w_hab", [128, 3, D])
        be1c_col = sb("be1c_col", [128, 1])
        be1c_r = sb("be1c_r", [128, D])
        bias_hl = sb("bias_hl", [128, 4, D], F32R)
        rowmask = sb("rowmask", [128, 4, 4])
        gconst = sb("gconst", [128, 4, D])
        grow = sb("grow", [128, 2, D])
        be2_bc = sb("be2_bc", [128, 128])
        wc = sb("wc", [128, D])
        v_r = sb("v_r", [128, D])
        ones_a = sb("ones_a", [128, N])
        ones_b = sb("ones_b", [128, N])
        newton_c = sb("newton_c", [128, 3, N])
        eps = sb("eps", [128, 1])
        offdiag = sb("offdiag", [128, N])
        pmask = sb("pmask", [128, 4])
        sel = sb("sel", [128, 32])
        lstage = sb("lstage", [128, 16 * N])

        xin = sb("xin", [128, RING, D])
        adjin = sb("adjin", [128, 2, N])
        xT = sb("xT", [128, 128])
        ab_hl = sb("ab_hl", [128, 2, 2, D], F32R)
        abT = sb("abT", [128, 2, 128])
        sq = sb("sq", [128, 2, 128])
        ve = sb("ve", [128, N])
        y = sb("y", [128, N])
        nt = sb("nt", [128, 2, N])
        std = sb("std", [128, N])
        s_hl = sb("s_hl", [128, 4, N], F32R)
        rw = sb("rw", [128, 2, 32, 2, 2])
        rwT = sb("rwT", [128, 4, 32])
        sumw = sb("sumw", [128, 2])
        hx = sb("hx", [128, RING, D])
        vw = sb("vw", [128, 2, D])
        hx2 = sb("hx2", [128, RING, D])
        xb = sb("xb", [128, RING, D])

        gmov = [sb(f"gmov{n}", [128, 4, 4 * D], F32R) for n in range(2)]
        lsta = [sb(f"lsta{n}", [128, 2, 16 * N], F32R) for n in range(2)]
        rwa = [sb(f"rwa{n}", [128, 4, 32]) for n in range(2)]
        wsel = [sb(f"wsel{n}", [128, UNITS * TILES, SLOT]) for n in range(2)]
        z = sb("z", [128, GELU_RING, TILES, D])
        g = sb("g", [128, GELU_RING, TILES, D])

        ms = sb("ms", [128, D])
        mT = sb("mT", [128, 128])
        hpre = sb("hpre", [128, D])
        stats = sb("stats", [128, 6])
        mv = sb("mv", [128, 2])
        vpe = sb("vpe", [128, 1])
        minus_half = sb("minus_half", [128, 1])
        rstd = sb("rstd", [128, 1])
        n1 = sb("n1", [128, D])
        g2T = sb("g2T", [128, 128])
        outs = sb("outs", [128, 2, D])

        up = [pb(f"up{n}", [128, TILES, D]) for n in range(2)]
        msg = [pb(f"msg{n}", [128, 512]) for n in range(2)]
        p0 = pb("p0", [128, 512])
        p1 = pb("p1", [128, 512])

        first_in, weights_in = sem("first_in"), sem("weights_in")
        ident_done, pool_const = sem("ident_done"), sem("pool_const")
        lstage_done, lsta_const, gmov_const = sem("lstage_done"), sem("lsta_const"), sem("gmov_const")
        centred, fold_in = sem("centred"), sem("fold_in")
        we2T_full, we2T_done = sem("we2T_full"), sem("we2T_done")
        fold_full, fold_done = sem("fold_full"), sem("fold_done")
        x_in = [sem(f"x_in{n}") for n in range(RING)]
        adj_in = [sem(f"adj_in{n}") for n in range(2)]
        ab_stored = sem("ab_stored")
        s_stored = sem("s_stored")
        w_stored = sem("w_stored")
        g_in = [sem(f"g_in{n}") for n in range(2)]
        l_in = [sem(f"l_in{n}") for n in range(2)]
        rwa_in = [sem(f"rwa_in{n}") for n in range(2)]
        out_stored = [sem(f"out_stored{n}") for n in range(2)]
        xT_full, xT_done = sem("xT_full"), sem("xT_done")
        ab_full, hi_done, lo_done = sem("ab_full"), sem("hi_done"), sem("lo_done")
        abT_full, abT_done, sq_done = sem("abT_full"), sem("abT_done"), sem("sq_done")
        v_full, ve_done, y_done = sem("v_full"), sem("ve_done"), sem("y_done")
        r_done, s_done, w_done = sem("r_done"), sem("s_done"), sem("w_done")
        rw_full, rwT_done = sem("rw_full"), sem("rwT_done")
        vw_done, hx2_done = sem("vw_done"), sem("hx2_done")
        xb_done, wsel_done = sem("xb_done"), sem("wsel_done")
        u_full, z_done, g_done, sum_done = sem("u_full"), sem("z_done"), sem("g_done"), sem("sum_done")
        ms_done, mT_full, mT_done = sem("ms_done"), sem("mT_full"), sem("mT_done")
        h_full, h_read, mv_done, rstd_done = sem("h_full"), sem("h_read"), sem("mv_done"), sem("rstd_done")
        n1_done, n1T_full, g2_done = sem("n1_done"), sem("n1T_full"), sem("g2_done")
        y_full, out_done = sem("y_full"), sem("out_done")
        s_hi = sem("s_hi")
        dve_step, pool_step = sem("dve_step"), sem("pool_step")
        dve_stats, pool_newton, pool_hx, pool_rstd = (
            sem("dve_stats"), sem("pool_newton"), sem("pool_hx"), sem("pool_rstd"))

        x_v = x.rearrange("(k par) i f -> k (par i) f", par=2)
        adj_v = adj.rearrange("(k par) i j -> k (par i) j", par=2)
        out_v = out.rearrange("(k par) i f -> k (par i) f", par=2)

        def at(view, k):
            if not k.looped:
                return view[k.c]
            v = view[bass.ds(k.number(), 1)]
            names = " ".join("abcdef"[: len(view.shape) - 1])
            return v.rearrange(f"z {names} -> (z {names.split()[0]}) {' '.join(names.split()[1:])}")

        def row(v):
            return v.unsqueeze(0).to_broadcast([128, D])

        def col(v):
            return v.rearrange("(p o) -> p o", o=1)

        first_weights = ((w1[:, 0], We1[0:D]), (w1[:, 1], We1[D:2 * D]), (be1_r, row(be1)), (ge_r, row(ge)),
                         (cols[:, 0:1], col(be1)), (wn1[:, 0], Wn1[0:D]), (bge_r, row(bge)))
        later_weights = ((we2[:], We2), (wn1[:, 1], Wn1[D:2 * D]), (cols[:, 3:4], col(be2)), (bn1_r, row(bn1)),
                         (bn2_r, row(bn2)), (wn2[:], Wn2), (cols[:, 1:2], col(gn)), (cols[:, 2:3], col(bgn)))
        ALL_FIRST, ALL_LATER = 16 * len(first_weights), 16 * len(later_weights)

        block = ctx.enter_context(nc.Block())

        @block.sync
        def _(sp):
            def load_x(k):
                if k.looped or k.c >= RING:
                    sp.wait_ge(xb_done, (k - RING).count())
                sp.dma_start(xin[:, k.ring(RING), :], at(x_v, k)).then_inc(x_in[k.ring(RING)], 16)

            def load_adj(k):
                if k.looped or k.c >= 2:
                    sp.wait_ge(w_done, (k - 2).count())
                sp.dma_start(adjin[:, k.ring(2), :], at(adj_v, k)).then_inc(adj_in[k.ring(2)], 16)

            def load_g(k):
                if k.looped or k.c >= 2:
                    sp.wait_ge(z_done, (k - 2).unit_count(UNITS - 1))
                if not k.looped:
                    sp.wait_ge(gmov_const, 1)
                    sp.wait_ge(lsta_const, 2)
                    sp.wait_ge(ab_stored, k.count(64))
                gv = gmov[k.ring(2)][:].bitcast(F32)
                for hl in range(2):
                    src = at(store_b, k)[hl].rearrange("(par jl h) x -> jl h par x", par=2, h=2)
                    dst = gv[K_B + 32 * hl:K_B + 32 * hl + 32].rearrange("q (h par) x -> q h par x", h=2)
                    sp.dma_start(dst, src).then_inc(g_in[k.ring(2)], 16)
                src = at(store_a, k).rearrange("q par tl f -> q (par tl f)").unsqueeze(1)
                sp.dma_start(gv[K_A:K_S].rearrange("q (h par) x -> q h (par x)", h=2),
                             src.to_broadcast([32, 2, 2 * 4 * D])).then_inc(g_in[k.ring(2)], 16)

            def load_s(k):
                sp.wait_ge(s_stored, k.count(16))
                lv = lsta[k.ring(2)][:].bitcast(F32)
                sv = at(store_s, k)
                for par in range(2):
                    sp.dma_start(lv[K_S:K_E, par],
                                 sv[:, par].rearrange("c (tl r) j -> c tl (r j)", tl=4)).then_inc(l_in[k.ring(2)], 16)

            def store_rw(k):
                sp.wait_ge(rwT_done, k.count())
                sp.dma_start(at(store_w, k).rearrange("p q e -> q p e"), rwT[:]).then_inc(w_stored, 16)

            def load_rw(k):
                if not k.looped and k.c >= 2:
                    sp.wait_ge(wsel_done, (k - 2).count())
                sp.wait_ge(w_stored, k.count(16))
                sp.dma_start(rwa[k.ring(2)][:].rearrange("q a e -> q (a e)"),
                             at(store_w, k).rearrange("p (jl a) e -> (p jl) (a e)", a=4)).then_inc(rwa_in[k.ring(2)], 16)

            def store_ab(k):
                sp.wait_ge(lo_done, k.count())
                for hl in range(2):
                    dst = at(store_a, k)[16 * hl:16 * hl + 16].rearrange("r par tl f -> (par tl) r f")
                    sp.dma_start(dst, ab_hl[:, hl, 0].bitcast(F32)).then_inc(ab_stored, 16)
                    sp.dma_start(at(store_b, k)[hl].rearrange("q (t f) -> q t f", t=4),
                                 ab_hl[:, hl, 1].bitcast(F32).unsqueeze(1).to_broadcast([128, 4, D])
                                 ).then_inc(ab_stored, 16)

            def store_std(k):
                sp.wait_ge(s_done, k.count())
                sp.dma_start(at(store_s, k).rearrange("c par i j -> (par i) c j"),
                             s_hl[:].bitcast(F32)).then_inc(s_stored, 16)

            def store_out(k):
                sp.wait_ge(out_done, k.count())
                sp.dma_start(at(out_v, k), outs[:, k.ring(2), :]).then_inc(out_stored[k.ring(2)], 16)

            for dst, src in first_weights:
                sp.dma_start(dst, src).then_inc(first_in, 16)
            load_x(Pair(0))
            load_adj(Pair(0))
            load_x(Pair(1))
            for dst, src in later_weights:
                sp.dma_start(dst, src).then_inc(weights_in, 16)
            load_x(Pair(2))
            load_adj(Pair(1))
            load_x(Pair(3))
            store_ab(Pair(0))
            load_g(Pair(0))
            store_ab(Pair(1))
            store_rw(Pair(0))
            store_std(Pair(0))
            load_rw(Pair(0))
            load_s(Pair(0))
            load_adj(Pair(2))
            store_ab(Pair(2))
            store_std(Pair(1))

            def iteration(k):
                if (k + 1).exists():
                    load_g(k + 1)
                    store_rw(k + 1)
                    load_s(k + 1)
                if (k + 4).exists():
                    load_x(k + 4)
                if (k + 3).exists():
                    load_adj(k + 3)
                if (k + 1).exists():
                    load_rw(k + 1)
                if (k + 3).exists():
                    store_ab(k + 3)
                if (k + 2).exists():
                    store_std(k + 2)
                if (k - 2).exists():
                    store_out(k - 2)

            schedule(sp, iteration)
            for n in range(2):
                sp.wait_ge(out_stored[n], PAIRS // 2 * 16)

        @block.gpsimd
        def _(pool):
            steps = [0]

            def link(ins):
                steps[0] += 1
                ins.then_inc(pool_step, 1)
                pool.wait_ge(pool_step, steps[0])

            def select(view, base, pattern):
                link(nc.gpsimd.affine_select(out=view, in_=view, compare_op=ALU.not_equal, fill=1.0,
                                             base=base, pattern=pattern, channel_multiplier=1))

            link(nc.gpsimd.memset(ident[:], 0.0))
            nc.gpsimd.affine_select(out=ident[:], in_=ident[:], compare_op=ALU.not_equal, fill=1.0, base=0,
                                    pattern=[[-1, 128]], channel_multiplier=1).then_inc(ident_done, 1)
            for view, value in ((ones_a, 1.0 / D), (ones_b, 64.0 * 64.0 / D), (eps, EPS),
                                (minus_half, -0.5), (offdiag, 1.0), (rowmask, 0.0)):
                nc.gpsimd.memset(view[:], value)
            for n, c in enumerate(NEWTON_C):
                last = nc.gpsimd.memset(newton_c[:, n], 3 * c * c)
            link(last)
            for par in range(2):
                v = offdiag[64 * par:64 * par + 64, :]
                link(nc.gpsimd.affine_select(out=v, in_=v, compare_op=ALU.not_equal, fill=0.0, base=0,
                                             pattern=[[-1, N]], channel_multiplier=1))
            for m, offs in ((0, (0, 8)), (1, (4, 12))):
                for off in offs:
                    select(rowmask[96:128, m, :], -off, [[-1, 4]])
            for m, off in ((2, 16), (3, 17)):
                select(rowmask[96:128, m, :], -off, [[0, 4]])
            nc.gpsimd.memset(pmask[:], 0.0).then_inc(pool_const, 1)
            pool.wait_ge(pool_const, 1)
            for p in range(4):
                link(nc.gpsimd.memset(pmask[32 * p:32 * p + 32, p:p + 1], 1.0))
            nc.gpsimd.memset(wsel[0][:], 0.0)
            link(nc.gpsimd.memset(wsel[1][:], 0.0))

            def squares(k):
                pool.wait_ge(abT_done, k.count())
                if (k - 1).exists():
                    pool.wait_ge(v_full, (k - 1).count())
                nc.gpsimd.tensor_tensor(sq[:], abT[:], abT[:], ALU.mult).then_inc(sq_done, 1)

            def newton(k):
                pool.wait_ge(y_done, k.count())
                done = 0

                def step(ins):
                    nonlocal done
                    done += 1
                    ins.then_inc(pool_newton, 1)
                    pool.wait_ge(pool_newton, (k - 1).count(12) + done)

                def by_h(v):
                    return v.rearrange("q (jl h) -> q jl h", h=2)

                r_new = rw[:, k.ring(2), :, 0, :]
                for n in range(3):
                    step(nc.gpsimd.tensor_tensor(nt[:, 0], y[:], y[:], ALU.mult))
                    step(nc.gpsimd.tensor_tensor(nt[:, 1], nt[:, 0], ve[:], ALU.mult))
                    step(nc.gpsimd.tensor_tensor(nt[:, 0], newton_c[:, n], nt[:, 1], ALU.subtract))
                    if n < 2:
                        step(nc.gpsimd.tensor_tensor(y[:], y[:], nt[:, 0], ALU.mult))
                if (k - 1).exists():
                    if (k - 2).exists() or k.looped:
                        pool.wait_ge(rw_full, (k - 2).count())
                    pool.wait_ge(s_stored, (k - 1).count(16))
                nc.gpsimd.tensor_tensor(r_new, by_h(y[:]), by_h(nt[:, 0]), ALU.mult).then_inc(r_done, 1)
                pool.wait_ge(r_done, k.count())
                nc.gpsimd.tensor_tensor(by_h(std[:]), by_h(ve[:]), r_new, ALU.mult).then_inc(pool_newton, 1)
                for twice in range(2):
                    last = nc.gpsimd.tensor_tensor(by_h(s_hl[:, twice]), by_h(ve[:]), r_new, ALU.mult)
                last.then_inc(s_hi, 1)
                pool.wait_ge(pool_newton, k.count(12))
                pool.wait_ge(s_hi, k.count())
                nc.gpsimd.tensor_tensor(s_hl[:, 2:4], std[:].unsqueeze(1).to_broadcast([128, 2, N]),
                                        s_hl[:, 0:2].bitcast(F32), ALU.subtract).then_inc(s_done, 1)

            def node_bias(k):
                pool.wait_ge(vw_done, k.count())
                v = vw[:, k.ring(2), :]
                nc.gpsimd.tensor_tensor(v, v, bn1_r, ALU.add).then_inc(pool_hx, 1)
                pool.wait_ge(pool_hx, k.count())
                if (k - RING).exists() or k.looped:
                    pool.wait_ge(h_read, (k - RING).count())
                nc.gpsimd.tensor_tensor(hx2[:, k.ring(RING), :], hx[:, k.ring(RING), :], v,
                                        ALU.add).then_inc(hx2_done, 1)

            def select_weights(k):
                pool.wait_ge(rwa_in[k.ring(2)], k.count2(16))
                if (k - 2).exists() or k.looped:
                    pool.wait_ge(sum_done, (k - 2).unit_count(UNITS - 1))
                w = rwa[k.ring(2)][:, 2:4, :].rearrange("q h e -> q (h e)")
                nc.gpsimd.tensor_tensor(wsel[k.ring(2)][:, :, 0:4],
                                        w.unsqueeze(2).to_broadcast([128, UNITS * TILES, 4]),
                                        pmask[:].unsqueeze(1).to_broadcast([128, UNITS * TILES, 4]),
                                        ALU.mult).then_inc(wsel_done, 1)

            def residual(k):
                pool.wait_ge(x_in[k.ring(RING)], k.count4(16))
                pool.wait_ge(xT_full, k.count())
                if (k - RING).exists() or k.looped:
                    pool.wait_ge(out_done, (k - RING).count())
                nc.gpsimd.tensor_tensor(xb[:, k.ring(RING), :], xin[:, k.ring(RING), :], bn2_r,
                                        ALU.add).then_inc(xb_done, 1)

            def node_rstd(k):
                pool.wait_ge(mv_done, k.count())
                nc.gpsimd.tensor_tensor(vpe[:], mv[:, 1:2], eps[:], ALU.add).then_inc(pool_rstd, 1)
                pool.wait_ge(pool_rstd, k.count())
                if (k - 1).exists():
                    pool.wait_ge(n1_done, (k - 1).count())
                nc.gpsimd.tensor_tensor(rstd[:], vpe[:], minus_half[:], ALU.pow).then_inc(rstd_done, 1)

            def normalise(k):
                node_rstd(k)
                pool.wait_ge(rstd_done, k.count())
                if (k - 1).exists():
                    pool.wait_ge(n1T_full, (k - 1).count())
                nc.gpsimd.tensor_tensor(n1[:], hpre[:], rstd[:].to_broadcast([128, D]), ALU.mult).then_inc(n1_done, 1)

            squares(Pair(0))
            newton(Pair(0))
            squares(Pair(1))
            newton(Pair(1))
            squares(Pair(2))
            select_weights(Pair(0))
            pool.wait_ge(weights_in, ALL_LATER)
            for c in range(2):
                node_bias(Pair(c))
                residual(Pair(c))

            def iteration(k):
                if (k - 2).exists():
                    normalise(k - 2)
                if (k + 2).exists():
                    newton(k + 2)
                if (k + 2).exists():
                    residual(k + 2)
                if (k + 3).exists():
                    squares(k + 3)
                if (k + 2).exists():
                    node_bias(k + 2)
                if (k + 1).exists():
                    select_weights(k + 1)

            schedule(pool, iteration)

        @block.scalar
        def _(act):
            def copy_xT(k):
                act.wait_ge(xT_full, k.count())
                if (k - 1).exists():
                    act.wait_ge(ab_full, (k - 1).count())
                    act.wait_ge(abT_full, (k - 1).count())
                nc.scalar.copy(xT[:], p1[:, 0:128]).then_inc(xT_done, 1)

            def high_parts(k):
                act.wait_ge(ab_full, k.count())
                if (k - 1).exists():
                    act.wait_ge(ab_stored, (k - 1).count(64))
                if (k - RING).exists() or k.looped:
                    act.wait_ge(hx2_done, (k - RING).count())
                nc.scalar.copy(hx[:, k.ring(RING), :], p0[:, 0:D])
                nc.scalar.copy(ab_hl[:, 0], p0[:, D:3 * D].rearrange("q (m f) -> q m f", m=2)).then_inc(hi_done, 1)

            def weigh_bias(k):
                act.wait_ge(w_done, k.count())
                if (k - 2).exists() or k.looped:
                    act.wait_ge(hx2_done, (k - 2).count())
                nc.scalar.activation(vw[:, k.ring(2), :], v_r[:], ACT.Identity,
                                     scale=sumw[:, k.ring(2):k.ring(2) + 1]).then_inc(vw_done, 1)

            def copy_abT(k):
                act.wait_ge(abT_full, k.count())
                if (k - 1).exists():
                    act.wait_ge(v_full, (k - 1).count())
                    act.wait_ge(sq_done, (k - 1).count())
                nc.scalar.activation(abT[:, 0], p1[:, 0:128], ACT.Identity, bias=be1c_col[:])
                nc.scalar.copy(abT[:, 1], p1[:, 128:256]).then_inc(abT_done, 1)

            def copy_rwT(k):
                act.wait_ge(rw_full, k.count())
                if (k - 1).exists():
                    act.wait_ge(w_stored, (k - 1).count(16))
                src = p1[:, 0:128].rearrange("q (pt tq p) -> q p tq pt", pt=8, tq=4)
                nc.scalar.copy(rwT[:].rearrange("q p (tq pt) -> q p tq pt", tq=4), src).then_inc(rwT_done, 1)

            def copy_messages(k):
                act.wait_ge(sum_done, k.unit_count(UNITS - 1))
                if (k - 1).exists():
                    act.wait_ge(mT_full, (k - 1).count())
                nc.scalar.copy(ms[:], msg[k.ring(2)][:, 0:D]).then_inc(ms_done, 1)

            def copy_mT(k):
                act.wait_ge(mT_full, k.count())
                if (k - 1).exists():
                    act.wait_ge(h_full, (k - 1).count())
                nc.scalar.copy(mT[:], p1[:, 0:128]).then_inc(mT_done, 1)

            def node_gelu(k):
                act.wait_ge(n1T_full, k.count())
                if (k - 1).exists():
                    act.wait_ge(y_full, (k - 1).count())
                nc.scalar.activation(g2T[:], p1[:, 0:128], ACT.Gelu, bias=cols[:, 2:3],
                                     scale=cols[:, 1:2]).then_inc(g2_done, 1)

            def edge_gelu(k, u):
                act.wait_ge(z_done, k.unit_count(u))
                nc.scalar.activation(g[:, u % GELU_RING], z[:, u % GELU_RING], ACT.Gelu).then_inc(g_done, 1)

            act.wait_ge(ident_done, 1)
            nc.scalar.activation(g[:, 0, 0, :], ident[:], ACT.Gelu)
            act.wait_ge(lstage_done, 1)
            nc.scalar.copy(lsta[1][:], lstage[:].unsqueeze(1).to_broadcast([128, 2, 16 * N])).then_inc(lsta_const, 1)
            copy_xT(Pair(0))
            act.wait_ge(centred, 1)
            copy_abT(Pair(0))
            high_parts(Pair(0))
            copy_xT(Pair(1))
            copy_abT(Pair(1))
            high_parts(Pair(1))
            copy_rwT(Pair(0))
            act.wait_ge(we2T_full, 1)
            nc.scalar.copy(we2T[:], p1[:, 0:128]).then_inc(we2T_done, 1)
            copy_xT(Pair(2))
            copy_abT(Pair(2))
            high_parts(Pair(2))
            act.wait_ge(weights_in, ALL_LATER)
            act.wait_ge(fold_done, 1)
            weigh_bias(Pair(0))
            weigh_bias(Pair(1))

            def iteration(k):
                for u in range(UNITS):
                    if k.exists():
                        edge_gelu(k, u)
                    if u == 0 and (k + 1).exists():
                        copy_rwT(k + 1)
                    if u == 0 and (k + 3).exists():
                        copy_xT(k + 3)
                    if u == 2 and (k - 1).exists():
                        copy_messages(k - 1)
                    if u == 3 and (k + 2).exists():
                        weigh_bias(k + 2)
                    if u == 3 and (k - 2).exists():
                        node_gelu(k - 2)
                    if u == 3 and (k + 3).exists():
                        high_parts(k + 3)
                    if u == 5 and (k - 1).exists():
                        copy_mT(k - 1)
                    if u == 7 and (k + 3).exists():
                        copy_abT(k + 3)

            schedule(act, iteration)

        @block.vector
        def _(dve):
            steps = [0]

            def link(ins):
                steps[0] += 1
                ins.then_inc(dve_step, 1)
                dve.wait_ge(dve_step, steps[0])

            def low_parts(k):
                dve.wait_ge(hi_done, k.count())
                nc.vector.tensor_tensor(ab_hl[:, 1], p0[:, D:3 * D].rearrange("q (m f) -> q m f", m=2),
                                        ab_hl[:, 0].bitcast(F32), ALU.subtract).then_inc(lo_done, 1)

            def weights(k):
                dve.wait_ge(adj_in[k.ring(2)], k.count2(16))
                if (k - 2).exists() or k.looped:
                    dve.wait_ge(rw_full, (k - 2).count())
                    dve.wait_ge(vw_done, (k - 2).count())
                nc.vector.scalar_tensor_tensor(
                    out=rw[:, k.ring(2), :, 1, :], in0=adjin[:, k.ring(2), :].rearrange("q (jl h) -> q jl h", h=2), scalar=1.0,
                    in1=offdiag[:].rearrange("q (jl h) -> q jl h", h=2), op0=ALU.mult, op1=ALU.mult,
                    accum_out=sumw[:, k.ring(2):k.ring(2) + 1]).then_inc(w_done, 1)

            def variance(k):
                dve.wait_ge(v_full, k.count())
                if (k - 1).exists():
                    dve.wait_ge(s_done, (k - 1).count())
                nc.vector.tensor_scalar(ve[:], p0[:, 0:N], 0.0, EPS, ALU.max, ALU.add).then_inc(ve_done, 1)

            def first_guess(k):
                dve.wait_ge(ve_done, k.count())
                nc.vector.tensor_scalar(y[:].bitcast(I32), ve[:].bitcast(I32), -0.5, float(RSQRT_MAGIC), ALU.mult,
                                        ALU.add).then_inc(y_done, 1)

            def node_sum(k):
                dve.wait_ge(h_full, k.count())
                dve.wait_ge(hx2_done, k.count())
                if (k - 1).exists():
                    dve.wait_ge(n1_done, (k - 1).count())
                nc.vector.tensor_tensor(hpre[:], p0[:, 0:D], hx2[:, k.ring(RING), :], ALU.add).then_inc(h_read, 1)

            def node_stats(k):
                dve.wait_ge(h_read, k.count())
                nc.vector.bn_stats(stats[:], hpre[:]).then_inc(dve_stats, 1)

            def weights_and_mean(k_w, k):
                if k.exists():
                    dve.wait_ge(dve_stats, k.count())
                if k_w.exists():
                    weights(k_w)
                if k.exists():
                    nc.vector.bn_aggr(mv[:], stats[:]).then_inc(mv_done, 1)

            def finish(k):
                dve.wait_ge(y_full, k.count())
                dve.wait_ge(xb_done, k.count())
                if (k - 2).exists() or k.looped:
                    dve.wait_ge(out_stored[k.ring(2)], (k - 2).count2(16))
                nc.vector.tensor_tensor(outs[:, k.ring(2), :], p0[:, 0:D], xb[:, k.ring(RING), :],
                                        ALU.add).then_inc(out_done, 1)

            def scale(k, u):
                dve.wait_ge(u_full, k.unit_count(u))
                if u == 0:
                    dve.wait_ge(rwa_in[k.ring(2)], k.count2(16))
                h, tq = divmod(u, 4)
                r = rwa[k.ring(2)][:, h, TILES * tq:TILES * (tq + 1)]
                nc.vector.tensor_tensor(z[:, u % GELU_RING], up[u % 2][:],
                                        r.unsqueeze(2).to_broadcast([128, TILES, D]), ALU.mult).then_inc(z_done, 1)

            dve.wait_ge(ident_done, 1)
            nc.vector.tensor_tensor(sel[0:64, 0:32], ident[0:64, 0:32], ident[0:64, 32:64], ALU.add)
            link(nc.vector.tensor_tensor(sel[64:96, 0:16], ident[64:96, 64:80], ident[64:96, 80:96], ALU.add))
            nc.vector.tensor_copy(lstage[0:64, :].rearrange("q (r jl h) -> q r jl h", jl=32, h=2),
                                  sel[0:64, 0:32].unsqueeze(1).unsqueeze(3).to_broadcast([64, 16, 32, 2]))
            nc.vector.tensor_copy(lstage[64:96, :].rearrange("q (r j) -> q r j", j=N),
                                  sel[64:96, 0:16].unsqueeze(2).to_broadcast([32, 16, N]))
            nc.vector.memset(lstage[96:128, :], 1.0).then_inc(lstage_done, 1)
            dve.wait_ge(lstage_done, 1)
            nc.vector.tensor_copy(lsta[0][:], lstage[:].unsqueeze(1).to_broadcast([128, 2, 16 * N])).then_inc(lsta_const, 1)
            dve.wait_ge(first_in, ALL_FIRST)
            nc.vector.reduce_sum(mean[:, 0:2], w1[:], axis=AXX)
            nc.vector.reduce_sum(mean[:, 3:4], wn1[:, 0], axis=AXX)
            link(nc.vector.reduce_sum(mean[:, 2:3], be1_r, axis=AXX))
            link(nc.vector.tensor_scalar(mean[:, 0:4], mean[:, 0:4], 1.0 / D, None, ALU.mult))
            nc.vector.tensor_scalar(w1[:, 1], w1[:, 1], mean[:, 1:2], None, ALU.subtract)
            nc.vector.tensor_scalar(w1c[:, 0], w1[:, 0], mean[:, 0:1], None, ALU.subtract)
            nc.vector.tensor_scalar(be1c_r[:], be1_r, mean[:, 2:3], None, ALU.subtract)
            link(nc.vector.tensor_scalar(be1c_col[:], cols[:, 0:1], mean[:, 2:3], None, ALU.subtract))
            nc.vector.tensor_scalar(w1c[:, 1], w1[:, 1], 1.0 / 64, None, ALU.mult)
            nc.vector.scalar_tensor_tensor(out=w_hab[:, 1], in0=w1c[:, 0], scalar=1 / R_SCALE, in1=ge_r,
                                           op0=ALU.mult, op1=ALU.mult)
            nc.vector.tensor_scalar(w_hab[:, 0], wn1[:, 0], mean[:, 3:4], None, ALU.subtract)
            nc.vector.scalar_tensor_tensor(out=w_hab[:, 2], in0=w1[:, 1], scalar=1 / R_SCALE, in1=ge_r,
                                           op0=ALU.mult, op1=ALU.mult).then_inc(centred, 1)
            nc.vector.tensor_scalar(bge_r, bge_r, 1 / R_SCALE ** 2, None, ALU.mult)
            link(nc.vector.scalar_tensor_tensor(out=be1c_r[:], in0=be1c_r[:], scalar=1 / R_SCALE, in1=ge_r,
                                                op0=ALU.mult, op1=ALU.mult))
            sources = ((0, bge_r), (2, be1c_r[:]))
            for m, src in sources:
                last = nc.vector.tensor_copy(bias_hl[:, m], src)
            link(last)
            for m, src in sources:
                nc.vector.tensor_tensor(bias_hl[:, m + 1], src, bias_hl[:, m].bitcast(F32), ALU.subtract)
            link(nc.vector.memset(sumw[:], 0.0))
            dve.wait_ge(pool_const, 1)
            weights(Pair(0))
            q = slice(K_S, 128)
            bias = [bias_hl[q, m].bitcast(F32) for m in range(4)]
            link(nc.vector.tensor_scalar(grow[q, 0], bias[2], rowmask[q, 2, 0:1], None, ALU.mult))
            link(nc.vector.scalar_tensor_tensor(out=grow[q, 1], in0=bias[3], scalar=rowmask[q, 3, 0:1],
                                                in1=grow[q, 0], op0=ALU.mult, op1=ALU.add))
            for m in range(2):
                for tl in range(4):
                    last = nc.vector.scalar_tensor_tensor(
                        out=gconst[q, tl], in0=bias[m], scalar=rowmask[q, m, tl:tl + 1],
                        in1=gconst[q, tl] if m else grow[q, 1], op0=ALU.mult, op1=ALU.add)
                link(last)
                if m == 0:
                    low_parts(Pair(0))
            variance(Pair(0))
            first_guess(Pair(0))
            for n in range(2):
                last = nc.vector.tensor_copy(
                    gmov[n][q], gconst[q].rearrange("q t f -> q (t f)").unsqueeze(1).to_broadcast([32, 4, 4 * D]))
            last.then_inc(gmov_const, 1)
            dve.wait_ge(weights_in, ALL_LATER)
            nc.vector.reduce_sum(mean[:, 4:5], wn1[:, 1], axis=AXX)
            link(nc.vector.reduce_sum(mean[:, 5:6], bn1_r, axis=AXX))
            link(nc.vector.tensor_scalar(mean[:, 4:6], mean[:, 4:6], 1.0 / D, None, ALU.mult))
            nc.vector.tensor_scalar(wn1[:, 1], wn1[:, 1], mean[:, 4:5], None, ALU.subtract)
            nc.vector.tensor_scalar(bn1_r, bn1_r, mean[:, 5:6], None, ALU.subtract)
            nc.vector.tensor_copy(be2_bc[:], cols[:, 3:4].to_broadcast([128, 128])).then_inc(fold_in, 1)
            low_parts(Pair(1))
            weights(Pair(1))
            variance(Pair(1))
            first_guess(Pair(1))
            dve.wait_ge(fold_full, 1)
            nc.vector.tensor_copy(wc[:], p0[:, 0:D])
            nc.vector.tensor_copy(v_r[:], p0[:, D:2 * D]).then_inc(fold_done, 1)
            low_parts(Pair(2))

            def iteration(k):
                for u in range(UNITS):
                    if k.exists():
                        scale(k, u)
                    if u == 0 and (k - 2).exists():
                        node_sum(k - 2)
                    if u == 1 and (k - 2).exists():
                        node_stats(k - 2)
                    if u == 1:
                        weights_and_mean(k + 2, k - 2)
                    if u == 2 and (k + 2).exists():
                        variance(k + 2)
                    if u == 3 and (k + 2).exists():
                        first_guess(k + 2)
                    if u == 5 and (k + 3).exists():
                        low_parts(k + 3)
                    if u == 7 and (k - 2).exists():
                        finish(k - 2)

            schedule(dve, iteration)

        @block.tensor
        def _(pe):
            def transpose_x(k, free=None):
                pe.wait_ge(x_in[k.ring(RING)], k.count4(16))
                if free:
                    pe.wait_ge(*free)
                nc.tensor.transpose(p1[:, 0:128], xin[:, k.ring(RING), :], ident[:]).then_inc(xT_full, 1)

            def node_products(k, free=None):
                pe.wait_ge(xT_done, k.count())
                if free:
                    pe.wait_ge(*free)
                nc.tensor.matmul(p0[:, 0:3 * D], xT[:], w_hab[:].rearrange("q a f -> q (a f)"),
                                 start=True, stop=True).then_inc(ab_full, 1)

            def feature_products(k, free=None):
                pe.wait_ge(xT_done, k.count())
                if free:
                    pe.wait_ge(*free)
                nc.tensor.matmul(p1[:, 0:128], w1c[:, 0], xT[:], start=True, stop=True)
                nc.tensor.matmul(p1[:, 128:256], w1c[:, 1], xT[:], start=True, stop=True).then_inc(abT_full, 1)

            def variances(k, free):
                pe.wait_ge(sq_done, k.count())
                pe.wait_ge(*free)
                terms = ((lambda s: abT[:, 0, s], lambda s: abT[:, 1, s]),
                         (lambda s: sq[:, 0, s], lambda s: ones_a[:]),
                         (lambda s: ones_b[:], lambda s: sq[:, 1, s]))
                for t, (left, right) in enumerate(terms):
                    for par in range(2):
                        s = slice(64 * par, 64 * par + 64)
                        last = nc.tensor.matmul(p0[s, 0:N], left(s), right(s), start=(t == 0), stop=(t == 2))
                last.then_inc(v_full, 1)

            def transpose_rw(k, free):
                pe.wait_ge(r_done, k.count())
                pe.wait_ge(w_done, k.count())
                if free:
                    pe.wait_ge(*free)
                nc.tensor.transpose(p1[:, 0:128], rw[:, k.ring(2)].rearrange("q jl a h -> q (jl a h)"), ident[:]).then_inc(rw_full, 1)

            def u_product(k, u):
                if u == 0:
                    pe.wait_ge(g_in[k.ring(2)], k.count2(48))
                    pe.wait_ge(l_in[k.ring(2)], k.count2(32))
                if k.looped or k.c * UNITS + u >= 2:
                    pe.wait_ge(z_done, k.unit_count(u - 2))
                h, tq = divmod(u, 4)
                for par in range(2):
                    selector = lsta[k.ring(2)][0:K_ROWS, par, 256 * tq:256 * tq + 256].rearrange("q (e h) -> q h e", h=2)
                    last = nc.tensor.matmul(up[u % 2][:, 4 * par:4 * par + 4, :].rearrange("q t f -> q (t f)"),
                                            selector[:, h],
                                            gmov[k.ring(2)][0:K_ROWS, 2 * h + par, :], start=True, stop=True)
                last.then_inc(u_full, 1)

            def weighted_sum(k, u):
                pe.wait_ge(g_done, k.unit_count(u))
                if u == 0:
                    pe.wait_ge(wsel_done, k.count())
                    if (k - 2).exists() or k.looped:
                        pe.wait_ge(ms_done, (k - 2).count())
                tq = u % 4
                ws = wsel[k.ring(2)][:].rearrange("q t s -> q (t s)")
                for tl0 in range(2):
                    for c in range(4):
                        tile = 4 * (c // 2) + 2 * (c % 2) + tl0
                        at0 = SLOT * (TILES * u + tile) - 16 * tl0 - 4 * tq
                        last = nc.tensor.matmul(msg[k.ring(2)][32 * c:32 * c + 32, 0:D], ws[:, at0:at0 + 32],
                                                g[:, u % GELU_RING, tile, :], start=(u == 0 and tl0 == 0),
                                                stop=(u == UNITS - 1 and tl0 == 1))
                last.then_inc(sum_done, 1)

            def transpose_messages(k, free):
                pe.wait_ge(ms_done, k.count())
                pe.wait_ge(*free)
                nc.tensor.transpose(p1[:, 0:128], ms[:], ident[:]).then_inc(mT_full, 1)

            def node_hidden(k, free):
                pe.wait_ge(mT_done, k.count())
                pe.wait_ge(*free)
                nc.tensor.matmul(p0[:, 0:D], mT[:], wc[:], start=True, stop=True).then_inc(h_full, 1)

            def transpose_n1(k, free):
                pe.wait_ge(n1_done, k.count())
                pe.wait_ge(*free)
                nc.tensor.transpose(p1[:, 0:128], n1[:], ident[:]).then_inc(n1T_full, 1)

            def node_output(k, free):
                pe.wait_ge(g2_done, k.count())
                pe.wait_ge(*free)
                nc.tensor.matmul(p0[:, 0:D], g2T[:], wn2[:], start=True, stop=True).then_inc(y_full, 1)

            pe.wait_ge(ident_done, 1)
            transpose_x(Pair(0))
            pe.wait_ge(centred, 1)
            feature_products(Pair(0), (xT_done, 1))
            pe.wait_ge(pool_const, 1)
            node_products(Pair(0))
            transpose_x(Pair(1), (abT_done, 1))
            variances(Pair(0), (lo_done, 1))
            feature_products(Pair(1), (xT_done, 2))
            node_products(Pair(1), (ve_done, 1))
            transpose_rw(Pair(0), (abT_done, 2))
            variances(Pair(1), (lo_done, 2))
            pe.wait_ge(weights_in, ALL_LATER)
            pe.wait_ge(rwT_done, 1)
            nc.tensor.transpose(p1[:, 0:128], we2[:], ident[:]).then_inc(we2T_full, 1)
            transpose_x(Pair(2), (we2T_done, 1))
            pe.wait_ge(ve_done, 2)
            pe.wait_ge(fold_in, 1)
            nc.tensor.matmul(p0[:, 0:D], we2T[:], wn1[:, 1], start=True, stop=True)
            nc.tensor.matmul(p0[:, D:2 * D], be2_bc[:], wn1[:, 1], start=True, stop=True).then_inc(fold_full, 1)
            feature_products(Pair(2), (xT_done, 3))
            node_products(Pair(2), (fold_done, 1))

            def iteration(k):
                nxt, two, three, prev, old = (k + 1).exists(), (k + 2).exists(), (k + 3).exists(), k - 1, k - 2
                for u in range(UNITS):
                    if k.exists():
                        u_product(k, u)
                    w = u - W_LAG
                    if w % 2:
                        of, w = (k, w) if w > 0 else (prev, w + UNITS)
                        if of.exists():
                            weighted_sum(of, w - 1)
                            weighted_sum(of, w)
                    if u == 0 and old.exists():
                        node_hidden(old, (out_done, (k - 3).count()) if (k - 3).exists()
                                         else (lo_done, (k + 2).count()))
                    if u == 1 and nxt:
                        transpose_rw(k + 1, (abT_done, (k + 2).count()) if two
                                            else (mT_done, old.count()))
                    if u == 2 and two:
                        variances(k + 2, (h_read, old.count()) if old.exists()
                                         else (lo_done, (k + 2).count()))
                    if u == 2 and three:
                        transpose_x(k + 3, (rwT_done, (k + 1).count()))
                    if u == 4 and three:
                        node_products(k + 3, (ve_done, (k + 2).count()))
                    if u == 4 and old.exists():
                        transpose_n1(old, (xT_done, (k + 3).count()) if three
                                          else (rwT_done, (k + 1).count()) if nxt
                                          else (mT_done, old.count()))
                    if u == 5 and prev.exists():
                        transpose_messages(prev, (g2_done, old.count()) if old.exists()
                                                 else (xT_done, (k + 3).count()))
                    if u == 7 and old.exists():
                        node_output(old, (lo_done, (k + 3).count()) if three
                                         else (ve_done, (k + 2).count()) if two
                                         else (h_read, old.count()))
                    if u == 7 and three:
                        feature_products(k + 3, (mT_done, prev.count()) if prev.exists()
                                                else (xT_done, (k + 3).count()))

            schedule(pe, iteration)


_WEIGHTS = ['We1', 'be1', 'ge', 'bge', 'We2', 'be2', 'Wn1', 'bn1', 'gn', 'bgn', 'Wn2', 'bn2']


def kernel(x, adj, **weights):
    import concourse.bacc as _bacc
    from concourse.bass_utils import run_bass_kernel_spmd as _run

    given = {"x": x, "adj": adj} | {name: weights[f"L0_gnn_{name}"] for name in _WEIGHTS}
    nc = _bacc.Bacc("TRN2", target_bir_lowering=False, num_devices=1)
    arrays, args = {}, []
    for name, a in given.items():
        a = np.ascontiguousarray(a)
        arrays[f"in_{name}"] = a
        args.append(nc.dram_tensor(f"in_{name}", a.shape, mybir.dt.from_np(a.dtype), kind="ExternalInput").ap())
    args.append(nc.dram_tensor("out_x", (B, N, D), F32, kind="ExternalOutput").ap())
    build(nc, *args)
    r = _run(nc, [arrays], core_ids=[0])
    return r.results[0]["out_x"]
```
